# Optimizing a Trainium2 kernel written in Bass

```python
import numpy as np
import jax
import jax.numpy as jnp

def _softmax(x, axis=-1):
    return jax.nn.softmax(x, axis=axis)

def _gelu(x):
    return jax.nn.gelu(x, approximate=True)

def _silu(x):
    return jax.nn.silu(x)

def _sigmoid(x):
    return jax.nn.sigmoid(x)

def _layernorm(x, axis=-1, eps=1e-05):
    m = jnp.mean(x, axis=axis, keepdims=True)
    v = jnp.var(x, axis=axis, keepdims=True)
    return (x - m) / jnp.sqrt(v + eps)

def _scatter_add(tgt, idx, src, axis=0):
    return tgt.at[idx].add(src)

def _segment_sum(src, seg, n):
    return jax.ops.segment_sum(src, seg, n)
kernel_name = 'mk_sandwich_d1_jaxref_r8_35c113'

def setup_inputs(seed: int=0):
    np.random.seed(seed)
    _w = jnp.asarray

    def _L0_attn_setup():
        import jax, jax.numpy as jnp
        import numpy as np
        DIM = 128
        NUM_HEADS = 16
        HEAD_DIM = DIM // NUM_HEADS
        EPS = 1e-06

        def _xavier(key, shape, gain=0.1):
            fan_in, fan_out = (shape[1], shape[0])
            limit = gain * np.sqrt(6.0 / (fan_in + fan_out))
            return jax.random.uniform(key, shape, jnp.float32, -limit, limit)

        def _phi(x):
            return jax.nn.elu(x) + 1.0
        key = jax.random.key(seed)
        kx, kq, kk, kv, ko = jax.random.split(key, 5)
        B, N = (4, 512)
        return {'x': jax.random.normal(kx, (B, N, DIM), jnp.float32), 'Wq': _xavier(kq, (DIM, DIM)), 'bq': jnp.zeros((DIM,), jnp.float32), 'Wk': _xavier(kk, (DIM, DIM)), 'bk': jnp.zeros((DIM,), jnp.float32), 'Wv': _xavier(kv, (DIM, DIM)), 'bv': jnp.zeros((DIM,), jnp.float32), 'Wo': _xavier(ko, (DIM, DIM)), 'bo': jnp.zeros((DIM,), jnp.float32)}
    _L0_attn_in = _L0_attn_setup()

    def _L0_ffn_setup():
        import jax, jax.numpy as jnp
        import numpy as np
        DIM = 128
        DEPTH = 6
        HEADS = 16
        DIM_HEAD = 64
        WINDOW = 32
        INNER = HEADS * DIM_HEAD
        DIM_INNER = int(DIM * 4 * 2 / 3)
        QK_SCALE = 8.0

        def shift_tokens(t):
            a, s = jnp.split(t, 2, -1)
            s = jnp.pad(s, ((0, 0), (1, 0), (0, 0)))[:, :-1]
            return jnp.concatenate([a, s], -1)

        def l2norm(t):
            return t / jnp.maximum(jnp.linalg.norm(t, axis=-1, keepdims=True), 1e-12)

        def rotate_half(x):
            x1, x2 = jnp.split(x, 2, -1)
            return jnp.concatenate([-x2, x1], -1)

        def rotary_tables(n):
            half = jnp.arange(0, DIM_HEAD, 2, dtype=jnp.float32)
            inv_freq = 1.0 / 10000.0 ** (half / DIM_HEAD)
            t = jnp.arange(n, dtype=jnp.float32)
            freqs = t[:, None] * inv_freq[None, :]
            freqs = jnp.concatenate([freqs, freqs], -1)
            base_scale = (half + 0.4 * DIM_HEAD) / (1.4 * DIM_HEAD)
            power = (t - n // 2) / (WINDOW // 2)
            scale = base_scale[None, :] ** power[:, None]
            scale = jnp.concatenate([scale, scale], -1)
            return (freqs, scale)

        def local_attention(q, k, v):
            b, h, n, d = q.shape
            w = WINDOW
            nw = n // w
            bq = q.reshape(b, h, nw, w, d)
            bk = k.reshape(b, h, nw, w, d)
            bv = v.reshape(b, h, nw, w, d)

            def look(t):
                p = jnp.pad(t, ((0, 0), (0, 0), (1, 0), (0, 0), (0, 0)))
                return jnp.concatenate([p[:, :, :nw], p[:, :, 1:]], axis=3)
            bk2, bv2 = (look(bk), look(bv))
            seq = jnp.arange(n).reshape(nw, w)
            seq_p = jnp.pad(seq, ((1, 0), (0, 0)), constant_values=-1)
            jt = jnp.concatenate([seq_p[:nw], seq_p[1:]], axis=1)
            it = seq[:, :, None]
            jb = jt[:, None, :]
            mask = (it < jb) | (it > jb + w) | (jb == -1)
            sim = jnp.einsum('bhwie,bhwje->bhwij', bq, bk2) * QK_SCALE
            sim = jnp.where(mask, -jnp.finfo(sim.dtype).max, sim)
            attn = jax.nn.softmax(sim, -1)
            out = jnp.einsum('bhwij,bhwje->bhwie', attn, bv2)
            return out.reshape(b, h, n, d)

        def attn_layer(x, Wqkv, qs, ksc, Wo):
            b, n, _ = x.shape
            qkv = x @ Wqkv
            q, k, v = jnp.split(qkv, 3, -1)
            sh = lambda t: t.reshape(b, n, HEADS, DIM_HEAD).transpose(0, 2, 1, 3)
            q, k, v = (sh(q), sh(k), sh(v))
            q = l2norm(q) * qs
            k = l2norm(k) * ksc
            freqs, scale = rotary_tables(n)
            cos, sin = (jnp.cos(freqs), jnp.sin(freqs))
            q = q * cos * scale + rotate_half(q) * sin * scale
            inv = 1.0 / scale
            k = k * cos * inv + rotate_half(k) * sin * inv
            out = local_attention(q, k, v)
            out = out.transpose(0, 2, 1, 3).reshape(b, n, INNER)
            return out @ Wo

        def ffn_layer(x, g, bln, W1, b1, W2, b2):
            mu = x.mean(-1, keepdims=True)
            var = ((x - mu) ** 2).mean(-1, keepdims=True)
            xn = (x - mu) / jnp.sqrt(var + 1e-05) * g + bln
            hg = xn @ W1 + b1
            a, gate = jnp.split(hg, 2, -1)
            return a * jax.nn.gelu(gate, approximate=False) @ W2 + b2
        key = jax.random.key(seed)
        ks = jax.random.split(key, 8)
        B, N = (2, 256)
        init = lambda k, shape: jax.random.normal(k, shape, jnp.float32) * 0.02
        return {'x': jax.random.normal(ks[0], (B, N, DIM), jnp.float32), 'Wqkv': init(ks[1], (DEPTH, DIM, 3 * INNER)), 'q_scale': jnp.ones((DEPTH, DIM_HEAD), jnp.float32), 'k_scale': jnp.ones((DEPTH, DIM_HEAD), jnp.float32), 'Wo': init(ks[2], (DEPTH, INNER, DIM)), 'ln_g': jnp.ones((DEPTH, DIM), jnp.float32), 'ln_b': jnp.zeros((DEPTH, DIM), jnp.float32), 'W1': init(ks[3], (DEPTH, DIM, 2 * DIM_INNER)), 'b1': jnp.zeros((DEPTH, 2 * DIM_INNER), jnp.float32), 'W2': init(ks[4], (DEPTH, DIM_INNER, DIM)), 'b2': jnp.zeros((DEPTH, DIM), jnp.float32)}
    _L0_ffn_in = _L0_ffn_setup()
    _d = {'L0_attn_x': _L0_attn_in['x'], 'L0_attn_Wq': _L0_attn_in['Wq'], 'L0_attn_bq': _L0_attn_in['bq'], 'L0_attn_Wk': _L0_attn_in['Wk'], 'L0_attn_bk': _L0_attn_in['bk'], 'L0_attn_Wv': _L0_attn_in['Wv'], 'L0_attn_bv': _L0_attn_in['bv'], 'L0_attn_Wo': _L0_attn_in['Wo'], 'L0_attn_bo': _L0_attn_in['bo'], 'L0_ffn_Wqkv': _L0_ffn_in['Wqkv'], 'L0_ffn_q_scale': _L0_ffn_in['q_scale'], 'L0_ffn_k_scale': _L0_ffn_in['k_scale'], 'L0_ffn_Wo': _L0_ffn_in['Wo'], 'L0_ffn_ln_g': _L0_ffn_in['ln_g'], 'L0_ffn_ln_b': _L0_ffn_in['ln_b'], 'L0_ffn_W1': _L0_ffn_in['W1'], 'L0_ffn_b1': _L0_ffn_in['b1'], 'L0_ffn_W2': _L0_ffn_in['W2'], 'L0_ffn_b2': _L0_ffn_in['b2']}
    _x0 = _d['L0_attn_x']
    _d['L0_attn_x'] = jax.random.normal(jax.random.fold_in(jax.random.key(seed), 1), (2, 1024, 128), dtype=_x0.dtype)
    del _x0
    return _d

def reference(L0_attn_x, L0_attn_Wq, L0_attn_bq, L0_attn_Wk, L0_attn_bk, L0_attn_Wv, L0_attn_bv, L0_attn_Wo, L0_attn_bo, L0_ffn_Wqkv, L0_ffn_q_scale, L0_ffn_k_scale, L0_ffn_Wo, L0_ffn_ln_g, L0_ffn_ln_b, L0_ffn_W1, L0_ffn_b1, L0_ffn_W2, L0_ffn_b2):

    def _L0_attn_ref(x, Wq, bq, Wk, bk, Wv, bv, Wo, bo):
        import jax, jax.numpy as jnp
        import numpy as np
        DIM = 128
        NUM_HEADS = 16
        HEAD_DIM = DIM // NUM_HEADS
        EPS = 1e-06

        def _xavier(key, shape, gain=0.1):
            fan_in, fan_out = (shape[1], shape[0])
            limit = gain * np.sqrt(6.0 / (fan_in + fan_out))
            return jax.random.uniform(key, shape, jnp.float32, -limit, limit)

        def _phi(x):
            return jax.nn.elu(x) + 1.0
        B, N, D = x.shape
        H, Hd = (NUM_HEADS, HEAD_DIM)
        Q = (x @ Wq.T + bq).reshape(B, N, H, Hd).transpose(0, 2, 1, 3)
        K = (x @ Wk.T + bk).reshape(B, N, H, Hd).transpose(0, 2, 1, 3)
        V = (x @ Wv.T + bv).reshape(B, N, H, Hd).transpose(0, 2, 1, 3)
        Q = _phi(Q)
        K = _phi(K)
        KV = jnp.einsum('bhnd,bhne->bhde', K, V)
        out = jnp.einsum('bhnd,bhde->bhne', Q, KV)
        Z = K.sum(axis=2)
        norm = jnp.einsum('bhnd,bhd->bhn', Q, Z)[..., None] + EPS
        out = out / norm
        out = out.transpose(0, 2, 1, 3).reshape(B, N, D)
        return out @ Wo.T + bo

    def _L0_ffn_ref(x, Wqkv, q_scale, k_scale, Wo, ln_g, ln_b, W1, b1, W2, b2):
        import jax, jax.numpy as jnp
        import numpy as np
        DIM = 128
        DEPTH = 6
        HEADS = 16
        DIM_HEAD = 64
        WINDOW = 32
        INNER = HEADS * DIM_HEAD
        DIM_INNER = int(DIM * 4 * 2 / 3)
        QK_SCALE = 8.0

        def shift_tokens(t):
            a, s = jnp.split(t, 2, -1)
            s = jnp.pad(s, ((0, 0), (1, 0), (0, 0)))[:, :-1]
            return jnp.concatenate([a, s], -1)

        def l2norm(t):
            return t / jnp.maximum(jnp.linalg.norm(t, axis=-1, keepdims=True), 1e-12)

        def rotate_half(x):
            x1, x2 = jnp.split(x, 2, -1)
            return jnp.concatenate([-x2, x1], -1)

        def rotary_tables(n):
            half = jnp.arange(0, DIM_HEAD, 2, dtype=jnp.float32)
            inv_freq = 1.0 / 10000.0 ** (half / DIM_HEAD)
            t = jnp.arange(n, dtype=jnp.float32)
            freqs = t[:, None] * inv_freq[None, :]
            freqs = jnp.concatenate([freqs, freqs], -1)
            base_scale = (half + 0.4 * DIM_HEAD) / (1.4 * DIM_HEAD)
            power = (t - n // 2) / (WINDOW // 2)
            scale = base_scale[None, :] ** power[:, None]
            scale = jnp.concatenate([scale, scale], -1)
            return (freqs, scale)

        def local_attention(q, k, v):
            b, h, n, d = q.shape
            w = WINDOW
            nw = n // w
            bq = q.reshape(b, h, nw, w, d)
            bk = k.reshape(b, h, nw, w, d)
            bv = v.reshape(b, h, nw, w, d)

            def look(t):
                p = jnp.pad(t, ((0, 0), (0, 0), (1, 0), (0, 0), (0, 0)))
                return jnp.concatenate([p[:, :, :nw], p[:, :, 1:]], axis=3)
            bk2, bv2 = (look(bk), look(bv))
            seq = jnp.arange(n).reshape(nw, w)
            seq_p = jnp.pad(seq, ((1, 0), (0, 0)), constant_values=-1)
            jt = jnp.concatenate([seq_p[:nw], seq_p[1:]], axis=1)
            it = seq[:, :, None]
            jb = jt[:, None, :]
            mask = (it < jb) | (it > jb + w) | (jb == -1)
            sim = jnp.einsum('bhwie,bhwje->bhwij', bq, bk2) * QK_SCALE
            sim = jnp.where(mask, -jnp.finfo(sim.dtype).max, sim)
            attn = jax.nn.softmax(sim, -1)
            out = jnp.einsum('bhwij,bhwje->bhwie', attn, bv2)
            return out.reshape(b, h, n, d)

        def attn_layer(x, Wqkv, qs, ksc, Wo):
            b, n, _ = x.shape
            qkv = x @ Wqkv
            q, k, v = jnp.split(qkv, 3, -1)
            sh = lambda t: t.reshape(b, n, HEADS, DIM_HEAD).transpose(0, 2, 1, 3)
            q, k, v = (sh(q), sh(k), sh(v))
            q = l2norm(q) * qs
            k = l2norm(k) * ksc
            freqs, scale = rotary_tables(n)
            cos, sin = (jnp.cos(freqs), jnp.sin(freqs))
            q = q * cos * scale + rotate_half(q) * sin * scale
            inv = 1.0 / scale
            k = k * cos * inv + rotate_half(k) * sin * inv
            out = local_attention(q, k, v)
            out = out.transpose(0, 2, 1, 3).reshape(b, n, INNER)
            return out @ Wo

        def ffn_layer(x, g, bln, W1, b1, W2, b2):
            mu = x.mean(-1, keepdims=True)
            var = ((x - mu) ** 2).mean(-1, keepdims=True)
            xn = (x - mu) / jnp.sqrt(var + 1e-05) * g + bln
            hg = xn @ W1 + b1
            a, gate = jnp.split(hg, 2, -1)
            return a * jax.nn.gelu(gate, approximate=False) @ W2 + b2
        for i in range(DEPTH):
            x = attn_layer(shift_tokens(x), Wqkv[i], q_scale[i], k_scale[i], Wo[i]) + x
            x = ffn_layer(shift_tokens(x), ln_g[i], ln_b[i], W1[i], b1[i], W2[i], b2[i]) + x
        return x
    x = L0_attn_x
    x = x + _layernorm(_L0_attn_ref(_layernorm(x, axis=-1), L0_attn_Wq, L0_attn_bq, L0_attn_Wk, L0_attn_bk, L0_attn_Wv, L0_attn_bv, L0_attn_Wo, L0_attn_bo), axis=-1)
    x = x + _layernorm(_L0_ffn_ref(_layernorm(x, axis=-1), L0_ffn_Wqkv, L0_ffn_q_scale, L0_ffn_k_scale, L0_ffn_Wo, L0_ffn_ln_g, L0_ffn_ln_b, L0_ffn_W1, L0_ffn_b1, L0_ffn_W2, L0_ffn_b2), axis=-1)
    return x

_drawn_inputs = setup_inputs


def setup_inputs(seed=0):
    import zlib

    import numpy as np

    out = dict(_drawn_inputs(seed))
    spreads = {'L0_attn_bq': (0.0, 2.0),
     'L0_attn_bk': (0.0, 2.0),
     'L0_attn_bv': (0.0, 0.1),
     'L0_attn_bo': (0.0, 0.1),
     'L0_ffn_q_scale': (1.0, 0.6),
     'L0_ffn_k_scale': (1.0, 0.6),
     'L0_ffn_ln_g': (1.0, 0.6),
     'L0_ffn_ln_b': (0.0, 0.8),
     'L0_ffn_b1': (0.0, 0.8),
     'L0_ffn_b2': (0.0, 0.368)}
    factors = {'L0_attn_Wq': 64.0,
     'L0_attn_Wk': 34.428,
     'L0_attn_Wv': 24.095,
     'L0_ffn_W1': 4.376,
     'L0_ffn_W2': 4.348}
    for name, (base, spread) in spreads.items():
        noise = np.random.default_rng([zlib.crc32(name.encode()), seed]).standard_normal(out[name].shape)
        drawn = base * np.exp(spread * noise) if base else spread * noise
        out[name] = jnp.asarray(drawn.astype(out[name].dtype))
    for name, factor in factors.items():
        out[name] = (out[name] * factor).astype(out[name].dtype)
    return out
```

```python
import concourse.bass as bass
from concourse import mybir
from concourse.alu_op_type import AluOpType as ALU
from contextlib import ExitStack

F32 = mybir.dt.float32
BF16 = mybir.dt.bfloat16
ACT = mybir.ActivationFunctionType
AX = mybir.AxisListType

P = 128
B, N = 2, 1024
TOK = B * N
TILES = TOK // P
TPB = TILES // B
CH = 512
CHUNKS = TOK // CH
CPB = CHUNKS // B
DEPTH, HEADS, HD, WIN = 6, 16, 64, 32
INNER = HEADS * HD
PAIRS = HEADS // 2
HALF = INNER // 2
FF = 341
FB = 114
FBLK = [(0, 114), (114, 114), (228, 113)]
NW = P // WIN
LA_HD = 8
LA_EPS, LN_EPS, L2_EPS = 1e-6, 1e-5, 1e-12
LN_PRE = 3 * CHUNKS
LN_FIN = LN_PRE + CHUNKS * DEPTH


def tcol(t):
    return t * P + t // TPB + 1


def ccol(c):
    return c * CH + c // CPB + 1


def program(nc, x, Wq, bq, Wk, bk, Wv, bv, Wo, bo, Wqkv, q_scale, k_scale, Wo6, ln_g, ln_b,
            W1, b1, W2, b2, c_mats, c_rot, c_mask, out):
    ctx = ExitStack()
    with ctx:
        def sb(name, shape, dt=F32):
            return ctx.enter_context(nc.sbuf_tensor(name, shape, dt))

        def sem(name):
            return ctx.enter_context(nc.semaphore(name))

        seeded = []

        def cnt(name):
            seeded.append(sem(name))
            return seeded[-1]

        def cnt2(name):
            return [cnt(f"{name}{i}") for i in range(2)]

        mats = sb("mats", [P, 4, P])
        ident, centre, blocks, ones_m = (mats[:, i, :] for i in range(4))
        ident_b = sb("ident_b", [P, P], BF16)
        mask_f = sb("mask_f", [P, 2, HD])
        mask = sb("mask", [P, TILES, HD], BF16)
        keep = sb("keep", [P, TILES])
        minus_half = sb("minus_half", [P, HEADS])
        rot_base = sb("rot_base", [P, TPB, 2, P])
        rot_tab = sb("rot_tab", [P, TPB, 2, P])
        scales = sb("scales", [P, 2, P])
        x1 = sb("x1", [P, TOK])
        xin = sb("xin", [P, TOK + B + 2])
        xmid = sb("xmid", [P, TOK + B + 2])
        wqkv = sb("wqkv", [P, 3 * INNER])
        wo = sb("wo", [P, PAIRS, P])
        w1 = sb("w1", [P, 2 * FF])
        w2 = sb("w2", [FB, 3, P])
        lng = sb("lng", [P, 1])
        lnb = sb("lnb", [P, 1])
        b1a = sb("b1a", [FB, 3])
        b1g = sb("b1g", [FB, 3])
        b2c = sb("b2c", [P, 1])
        xs = sb("xs", [P, 2, P])
        xsv = sb("xsv", [P, 2, P])
        sq = sb("sq", [P, 2, 2 * HALF])
        rotA = sb("rotA", [P, 2, 2 * HALF])
        rotB = sb("rotB", [P, 2, 2 * HALF])
        nsq = sb("nsq", [P, 2, HEADS])
        nrm = sb("nrm", [P, 2, HEADS])
        rinv = sb("rinv", [P, 2, HEADS])
        rq = sb("rq", [P, 2, HEADS])
        qT = sb("qT", [P, PAIRS, P])
        kT = sb("kT", [P, PAIRS, WIN + P])
        V = sb("V", [P, 2, INNER])
        prob = sb("prob", [P, HEADS, 2 * WIN])
        mx = sb("mx", [P, HEADS])
        ssum = sb("ssum", [P, HEADS])
        rsum = sb("rsum", [P, HEADS])
        PT = sb("PT", [P, HEADS, P])
        PTp = sb("PTp", [P, HEADS, WIN])
        oT = sb("oT", [P, PAIRS, P])
        ln_sqb = sb("ln_sqb", [P, CH])
        ln_xcb = sb("ln_xcb", [P, CH])
        ln_ve = sb("ln_ve", [P, 4])
        ln_r = sb("ln_r", [P, 4])
        xsf = sb("xsf", [P, CH])
        xn = sb("xn", [P, 2, CH])
        gl = sb("gl", [FB, 2, CH])
        hm = sb("hm", [FB, 3, CH])
        ps = ctx.enter_context(nc.psum_tensor("ps", [P, 8, CH], F32))

        wnat = rotB[:, 0, 0:512].rearrange("p (a n) -> p a n", a=4)
        wT = rotB[:, 0, 512:1024].rearrange("p (a n) -> p a n", a=4)
        bq_c, bo_c = rsum[:, 0:1], rsum[:, 1:2]
        bkv = sb("bkv", [P, 2, P])
        xst = sq[:, 0, 0:512].rearrange("p (i f) -> p i f", i=4)
        phiQ = wqkv[:, 0:2 * CH].rearrange("p (c n) -> p c n", c=2)
        relu_t = sq[:, 1, 0:512]
        min_t = sq[:, 1, 512:1024]
        kz = rotA[:, 0, 0:512]
        phiK = rotA[:, 0, 512:1024]
        Vo = wqkv[:, 1024:1024 + 4 * 130].rearrange("p (i n) -> p i n", i=4)
        KVbd = rotA[:, 1, 0:128]
        Zbd = rotA[:, 1, 128:256]
        rden = rotA[:, 1, 512:1024]
        att = rotB[:, 1, 0:512]
        ysb = rotB[:, 1, 512:1024]
        ost = sq[:, 0, 512:1024].rearrange("p (i f) -> p i f", i=4)

        s_const, s_bias, s_wla, s_x, s_out = map(sem, ["s_const", "s_bias", "s_wla", "s_x", "s_out"])
        s_wattn, s_wffn = sem("s_wattn"), sem("s_wffn")
        s_init = sem("s_init")
        init_v, init_p = sem("init_v"), sem("init_p")
        wT_done, wT_copied = sem("wT_done"), sem("wT_copied")
        xT_done, xT_copied = cnt("xT_done"), cnt("xT_copied")
        ln_cen, ln_sq, ln_var, ln_eps, ln_pow, ln_bc, ln_mul, ln_out = map(
            cnt, ["ln_cen", "ln_sq", "ln_var", "ln_eps", "ln_pow", "ln_bc", "ln_mul", "ln_out"])
        la_q, la_qmin, la_qexp, la_phiq = map(cnt, ["la_q", "la_qmin", "la_qexp", "la_phiq"])
        la_kv, la_kb, la_kmin, la_kexp, la_phik = map(cnt, ["la_kv", "la_kb", "la_kmin", "la_kexp", "la_phik"])
        la_sum, la_bd, la_num, la_den, la_rden, la_att, la_y, la_ysb, la_x1 = map(
            cnt, ["la_sum", "la_bd", "la_num", "la_den", "la_rden", "la_att", "la_y", "la_ysb", "la_x1"])
        tab_done = cnt("tab_done")
        xs_done, xsv_done = cnt("xs_done"), cnt("xsv_done")
        qk_done, sq_done, prod_done, nsq_done = map(cnt2, ["qk_done", "sq_done", "prod_done", "nsq_done"])
        add_done, kmul_done, r_done = map(cnt2, ["add_done", "kmul_done", "r_done"])
        pool_own = cnt("pool_own")
        nrm_done = cnt2("nrm_done")
        tq_done, tq_evac, tk_done, tk_evac = map(cnt2, ["tq_done", "tq_evac", "tk_done", "tk_evac"])
        kprev = cnt2("kprev")
        v_done, v_evac, av_done, o_evac = map(cnt2, ["v_done", "v_evac", "av_done", "o_evac"])
        s_done, scaled, mx_done, sub_done, exp_done, sum_done, rs_done, norm_done, pt_done, y_done, xmid_done = map(
            cnt, ["s_done", "scaled", "mx_done", "sub_done", "exp_done", "sum_done", "rs_done", "norm_done",
                  "pt_done", "y_done", "xmid_done"])
        xsf_done, h_done, gl_done, hm_done, f_done, xout_done = map(
            cnt, ["xsf_done", "h_done", "gl_done", "hm_done", "f_done", "xout_done"])
        fin_add, fin_T, fin_copied = map(cnt, ["fin_add", "fin_T", "fin_copied"])

        block = ctx.enter_context(nc.Block())

        @block.sync
        def _(sp):
            for counter in seeded:
                sp.sem_inc(counter, 1)
            sp.dma_start(mats[:], c_mats).then_inc(s_const, 16)
            sp.dma_start(wnat[:, 0, :], Wq).then_inc(s_wla, 16)
            sp.dma_start(wnat[:, 1, :], Wk).then_inc(s_wla, 16)
            sp.dma_start(wnat[:, 2, :], Wv).then_inc(s_wla, 16)
            sp.dma_start(wnat[:, 3, :], Wo).then_inc(s_wla, 16)
            sp.dma_start(mask_f[:], c_mask).then_inc(s_const, 16)
            sp.dma_start(rot_base[:], c_rot).then_inc(s_const, 16)
            sp.dma_start(bq_c, bq.rearrange("(p a) -> p a", a=1)).then_inc(s_bias, 16)
            sp.dma_start(bo_c, bo.rearrange("(p a) -> p a", a=1)).then_inc(s_bias, 16)
            sp.dma_start(bkv[:, 0, :], bk.partition_broadcast(P)).then_inc(s_bias, 16)
            sp.dma_start(bkv[:, 1, :], bv.partition_broadcast(P)).then_inc(s_bias, 16)
            xr = x.rearrange("b (c i p) f -> (b c) p i f", i=4, p=P)
            with sp.Fori(0, CHUNKS) as c:
                sp.wait_ge(xT_done, c + 1)
                sp.dma_start(xst, xr[bass.ds(c, 1), :, :, :].rearrange("a p i f -> (a p) i f")).then_inc(s_x, 16)
            sp.wait_ge(la_x1, CHUNKS + 1)
            with sp.Fori(0, DEPTH) as l:
                sp.wait_ge(v_done[1], l * TILES + 1)
                sp.dma_start(wqkv[:], Wqkv[bass.ds(l, 1), :, :].rearrange("a p n -> (a p) n")).then_inc(s_wattn, 16)
                sp.wait_ge(tab_done, l + 1)
                for qk, s in ((0, q_scale), (1, k_scale)):
                    row = s[bass.ds(l, 1), :].rearrange("a d -> (a d)")
                    o = qk * HD
                    sp.dma_start(scales[:, 0, o:o + HD], row.partition_broadcast(P)).then_inc(s_wattn, 16)
                    sp.dma_start(scales[:, 1, o:o + 32], row[32:64].partition_broadcast(P)).then_inc(s_wattn, 16)
                    sp.dma_start(scales[:, 1, o + 32:o + 64], row[0:32].partition_broadcast(P)).then_inc(s_wattn, 16)
                sp.wait_ge(y_done, l * TILES + 1)
                sp.dma_start(wo[:], Wo6[bass.ds(l, 1), :, :].rearrange("a (k p) n -> (a p) k n", p=P)).then_inc(s_wattn, 16)
                sp.wait_ge(xout_done, l * CHUNKS + 1)
                sp.dma_start(w1[:], W1[bass.ds(l, 1), :, :].rearrange("a p n -> (a p) n")).then_inc(s_wffn, 16)
                w2l = W2[bass.ds(l, 1), :, :].rearrange("a k n -> (a k) n")
                b1l = b1[bass.ds(l, 1), :].rearrange("a n -> (a n)")
                sp.dma_start(w2[:, 0:2, :], w2l[0:228, :].rearrange("(m k) n -> k m n", m=2)).then_inc(s_wffn, 16)
                sp.dma_start(w2[0:113, 2, :], w2l[228:341, :]).then_inc(s_wffn, 16)
                for dst, o in ((b1a, 0), (b1g, FF)):
                    sp.dma_start(dst[:, 0:2], b1l[o:o + 228].rearrange("(m k) -> k m", m=2),
                                 allow_slow_non_contiguous=True).then_inc(s_wffn, 16)
                    sp.dma_start(dst[0:113, 2:3], b1l[o + 228:o + 341].rearrange("(k a) -> k a", a=1)).then_inc(s_wffn, 16)
                for dst, src in ((lng, ln_g), (lnb, ln_b), (b2c, b2)):
                    sp.dma_start(dst[:], src[bass.ds(l, 1), :].rearrange("a (p q) -> (a p) q", q=1)).then_inc(s_wffn, 16)
            sp.sem_inc(s_out, 16)
            outr = out.rearrange("b (c i p) f -> (b c) p i f", i=4, p=P)
            with sp.Fori(0, CHUNKS) as c:
                sp.wait_ge(fin_copied, c + 2)
                sp.dma_start(outr[bass.ds(c, 1), :, :, :].rearrange("a p i f -> (a p) i f"), ost).then_inc(s_out, 16)
            sp.wait_ge(s_out, 16 * CHUNKS + 16)
        N_WATTN, N_WFFN = 8 * 16, 10 * 16

        @block.gpsimd
        def _(pool):
            gp = nc.gpsimd
            own = [0]

            gp.memset(minus_half[:], -0.5).then_inc(init_p, 1)
            gp.memset(PT[:], 0.0).then_inc(init_p, 1)
            gp.memset(kT[:], 0.0).then_inc(init_p, 1)
            gp.memset(V[:], 0.0).then_inc(init_p, 1)
            pool.wait_ge(init_p, 4)

            def ln(n):
                pool.wait_ge(ln_eps, n + 2)
                gp.tensor_tensor(ln_r[:], ln_ve[:], minus_half[:, 0:4], ALU.pow).then_inc(ln_pow, 1)

            with pool.Fori(0, B) as b:
                for cc in range(CPB):
                    c = b * CPB + cc
                    ln(b * 6 + cc)
                    pool.wait_ge(la_qexp, c + 2)
                    gp.tensor_tensor(phiQ[:, cc, :], relu_t, min_t, ALU.add).then_inc(la_phiq, 1)
                    pool.wait_ge(la_kexp, c + 2)
                    gp.tensor_tensor(phiK, relu_t, min_t, ALU.add).then_inc(la_phik, 1)
                for cc in range(CPB):
                    ln(b * 6 + 2 + 2 * cc)
                    ln(b * 6 + 3 + 2 * cc)

            def unit(l, t, p, h):
                pool.wait_ge(prod_done[h], l * TILES + t + 2)
                gp.tensor_tensor(rotA[:, h, :], rotA[:, h, :], rotB[:, h, :], ALU.add).then_inc(add_done[h], 1)
                pool.wait_ge(nsq_done[h], l * TILES + t + 2)
                gp.tensor_tensor(rinv[:, h, :], nsq[:, h, :], minus_half[:], ALU.pow).then_inc(pool_own, 1)
                pool.wait_ge(pool_own, (l * TILES + t) * 2 + h + 2)
                kk = rotA[:, h, HALF:].rearrange("p (a d) -> p a d", d=HD)
                gp.tensor_tensor(kk, kk, rinv[:, h, 8:16].unsqueeze(2).broadcast_to([P, 8, HD]),
                                 ALU.mult).then_inc(kmul_done[h], 1)
                gp.tensor_scalar(rq[:, p, 8 * h:8 * h + 8], rinv[:, h, 0:8], 8.0, None, ALU.mult).then_inc(r_done[h], 1)

            def slot(l, t, p, qk, mid, av):
                if qk:
                    unit(l, t, p, 0)
                if av:
                    pool.wait_ge(rs_done, l * TILES + t)
                    gp.tensor_tensor(prob[:], prob[:], rsum[:].unsqueeze(2).broadcast_to([P, HEADS, 2 * WIN]),
                                     ALU.mult).then_inc(norm_done, 1)
                if qk:
                    unit(l, t, p, 1)
                if mid:
                    pool.wait_ge(mx_done, l * TILES + t + 1)
                    gp.tensor_tensor(prob[:], prob[:], mx[:].unsqueeze(2).broadcast_to([P, HEADS, 2 * WIN]),
                                     ALU.subtract).then_inc(sub_done, 1)

            with pool.Fori(0, DEPTH) as l:
                pool.wait_ge(s_wattn, l * N_WATTN + N_WATTN)
                if True:
                    pool.wait_ge(s_const, 48)
                pool.wait_ge(prod_done[1], l * TILES + 1)
                for part in range(2):
                    ins = gp.tensor_tensor(rot_tab[:, :, part, :], rot_base[:, :, part, :],
                                           scales[:, part, :].unsqueeze(1).broadcast_to([P, TPB, P]), ALU.mult)
                ins.then_inc(tab_done, 1)
                slot(l, 0, 0, True, False, False)
                slot(l, 1, 1, True, True, False)
                with pool.Fori(0, TILES // 2 - 1) as j:
                    for p in range(2):
                        slot(l, 2 * j + 2 + p, p, True, True, True)
                slot(l, TILES, 0, False, True, True)
                slot(l, TILES + 1, 1, False, False, True)
                for c in range(CHUNKS):
                    ln(LN_PRE + l * CHUNKS + c)
            with pool.Fori(0, CHUNKS) as c:
                ln(LN_FIN + c)

        @block.scalar
        def _(act):
            ac = nc.scalar

            def ln(n):
                act.wait_ge(ln_cen, n + 2)
                act.wait_ge(ln_out, n + 1)
                ac.activation(ln_xcb[:], ps[:, 0, :], ACT.Copy)
                ac.activation(ln_sqb[:], ps[:, 0, :], ACT.Square).then_inc(ln_sq, 1)

            act.wait_ge(s_bias, 64)
            with act.Fori(0, B) as b:
                for cc in range(CPB):
                    c = b * CPB + cc
                    ln(b * 6 + cc)
                    act.wait_ge(la_q, c + 2)
                    act.wait_ge(la_phik, c + 1)
                    act.wait_ge(la_qmin, c + 2)
                    ac.activation(relu_t, ps[:, 4, :], ACT.Relu, bias=bq_c)
                    ac.activation(min_t, min_t, ACT.Exp).then_inc(la_qexp, 1)
                    act.wait_ge(la_phiq, c + 2)
                    act.wait_ge(la_kb, c + 2)
                    ac.activation(relu_t, kz, ACT.Relu)
                    act.wait_ge(la_kmin, c + 2)
                    ac.activation(min_t, min_t, ACT.Exp).then_inc(la_kexp, 1)
                for cc in range(CPB):
                    c = b * CPB + cc
                    act.wait_ge(la_y, c + 2)
                    act.wait_ge(ln_cen, b * 6 + 2 + 2 * cc + 1)
                    ac.activation(ysb, ps[:, 5, :], ACT.Identity, bias=bo_c).then_inc(la_ysb, 1)
                    ln(b * 6 + 2 + 2 * cc)
                    ln(b * 6 + 3 + 2 * cc)

            def sq_unit(l, t, h):
                act.wait_ge(qk_done[h], l * TILES + t + 2)
                act.wait_ge(nsq_done[h], l * TILES + t + 1)
                ac.activation(sq[:, h, :], ps[:, 0:2, :].rearrange("p a n -> p (a n)"), ACT.Square).then_inc(sq_done[h], 1)

            def evac_tq(l, t, h):
                act.wait_ge(tq_done[h], l * TILES + t + 2)
                act.wait_ge(s_done, l * TILES + t + 1)
                ac.activation(qT[:, 4 * h:4 * h + 4, :], ps[:, 3, :].rearrange("p (a n) -> p a n", a=4),
                              ACT.Copy).then_inc(tq_evac[h], 1)

            def evac_tk(l, t, h):
                ac.activation(kT[:, 4 * h:4 * h + 4, 0:WIN], kT[:, 4 * h:4 * h + 4, P:P + WIN], ACT.Copy,
                              scale=keep[:, bass.ds(t, 1)]).then_inc(kprev[h], 1)
                act.wait_ge(kprev[h], l * TILES + t + 2)
                act.wait_ge(tk_done[h], l * TILES + t + 2)
                ac.activation(kT[:, 4 * h:4 * h + 4, WIN:], ps[:, 3, :].rearrange("p (a n) -> p a n", a=4),
                              ACT.Copy).then_inc(tk_evac[h], 1)

            def evac_v(l, t, p, h):
                act.wait_ge(v_done[h], l * TILES + t + 2)
                act.wait_ge(av_done[1], l * TILES + t + 1)
                ac.activation(V[:, p, h * HALF:(h + 1) * HALF], ps[:, 2, :], ACT.Copy).then_inc(v_evac[h], 1)

            def evac_o(l, t, h):
                act.wait_ge(av_done[h], l * TILES + t + 2)
                act.wait_ge(y_done, l * TILES + t + 1)
                ac.activation(oT[:, 4 * h:4 * h + 4, :], ps[:, 6 + h, :].rearrange("p (a n) -> p a n", a=4),
                              ACT.Copy).then_inc(o_evac[h], 1)

            def slot(l, t, p, qk, mid, av):
                if av:
                    act.wait_ge(sub_done, l * TILES + t)
                    ac.activation(prob[:], prob[:], ACT.Exp).then_inc(exp_done, 1)
                if qk:
                    sq_unit(l, t, 0)
                if mid:
                    evac_tq(l, t - 1, 1)
                if av:
                    evac_v(l, t - 2, p, 0)
                if mid:
                    evac_tk(l, t - 1, 1)
                if av:
                    evac_v(l, t - 2, p, 1)
                if qk:
                    sq_unit(l, t, 1)
                    evac_tq(l, t, 0)
                if av:
                    evac_o(l, t - 2, 0)
                if qk:
                    evac_tk(l, t, 0)
                if av:
                    evac_o(l, t - 2, 1)

            act.wait_ge(init_p, 4)
            act.wait_ge(init_v, 5)
            with act.Fori(0, DEPTH) as l:
                slot(l, 0, 0, True, False, False)
                slot(l, 1, 1, True, True, False)
                with act.Fori(0, TILES // 2 - 1) as j:
                    for p in range(2):
                        slot(l, 2 * j + 2 + p, p, True, True, True)
                slot(l, TILES, 0, False, True, True)
                slot(l, TILES + 1, 1, False, False, True)
                act.wait_ge(s_wffn, l * N_WFFN + N_WFFN)
                ln(LN_PRE + l * CHUNKS)
                for c in range(CHUNKS):
                    if c + 1 < CHUNKS:
                        ln(LN_PRE + l * CHUNKS + c + 1)
                    for m, (_, fb) in enumerate(FBLK):
                        k = 3 * c + m
                        act.wait_ge(h_done, l * 12 + k + 2)
                        if k >= 2:
                            act.wait_ge(hm_done, l * 12 + k)
                        ac.activation(gl[0:fb, k % 2, :], ps[0:fb, 5 + k % 2, :], ACT.Gelu,
                                      bias=b1g[0:fb, m:m + 1]).then_inc(gl_done, 1)
            with act.Fori(0, CHUNKS) as c:
                ln(LN_FIN + c)

        @block.vector
        def _(dve):
            ve = nc.vector
            dve.wait_ge(s_const, 48)
            ve.tensor_copy(ident_b[:], ident)
            ve.tensor_copy(mask[:], mask_f[:, 1:2, :].broadcast_to([P, TILES, HD])).then_inc(init_v, 1)
            dve.wait_ge(init_v, 1)
            ve.tensor_copy(mask[:, 0:TILES:TPB, :], mask_f[:, 0:1, :].broadcast_to([P, B, HD])).then_inc(init_v, 1)
            ve.memset(keep[:], 1.0)
            ve.memset(xin[:], 0.0).then_inc(init_v, 1)
            ve.memset(xmid[:], 0.0).then_inc(init_v, 1)
            dve.wait_ge(init_v, 4)
            ve.memset(keep[:, 0:TILES:TPB], 0.0).then_inc(init_v, 1)

            def ln_a(n):
                dve.wait_ge(ln_var, n + 2)
                ve.tensor_scalar(ln_ve[:], ps[:, 1, 0:4], LN_EPS, None, ALU.add).then_inc(ln_eps, 1)

            def ln_b(n, dst, affine=False):
                dve.wait_ge(ln_bc, n + 2)
                if not affine:
                    ve.tensor_tensor(dst, ps[:, 2, :], ln_xcb[:], ALU.mult).then_inc(ln_out, 1)
                else:
                    ve.tensor_tensor(dst, ps[:, 2, :], ln_xcb[:], ALU.mult).then_inc(ln_mul, 1)
                    dve.wait_ge(ln_mul, n - LN_PRE + 2)
                    ve.tensor_scalar(dst, dst, lng[:], lnb[:], ALU.mult, ALU.add).then_inc(ln_out, 1)

            dve.wait_ge(wT_done, 1)
            ve.tensor_copy(wT, ps[:, 3, :].rearrange("p (a n) -> p a n", a=4)).then_inc(wT_copied, 1)
            dve.wait_ge(s_bias, 64)
            ve.memset(Vo[:, :, P:P + 2], 1.0)
            with dve.Fori(0, B) as b:
                for cc in range(CPB):
                    c = b * CPB + cc
                    n = b * 6 + cc
                    dve.wait_ge(xT_done, c + 2)
                    ve.tensor_copy(x1[:, bass.ds(c * CH, CH)], ps[:, 3, :]).then_inc(xT_copied, 1)
                    ln_a(n)
                    ln_b(n, xn[:, 0, :])
                    dve.wait_ge(la_q, c + 2)
                    dve.wait_ge(la_phik, c + 1)
                    ve.tensor_scalar(min_t, ps[:, 4, :], bq_c, 0.0, ALU.add, ALU.min).then_inc(la_qmin, 1)
                    dve.wait_ge(la_kv, c + 2)
                    kv = ps[:, 5:7, :].rearrange("p a (i n) -> p (a i) n", n=2 * P)
                    ve.tensor_tensor(kz.rearrange("p (i n) -> p i n", i=4), kv[:, :, 0:P],
                                     bkv[:, 0:1, :].broadcast_to([P, 4, P]), ALU.add).then_inc(la_kb, 1)
                    ve.tensor_tensor(Vo[:, :, 0:P], kv[:, :, P:],
                                     bkv[:, 1:2, :].broadcast_to([P, 4, P]), ALU.add)
                    dve.wait_ge(la_kb, c + 2)
                    dve.wait_ge(la_phiq, c + 2)
                    ve.tensor_scalar(min_t, kz, 0.0, None, ALU.min).then_inc(la_kmin, 1)
                dve.wait_ge(la_sum, b + 2)
                ve.tensor_tensor(KVbd, ps[:, 7, 0:P], blocks, ALU.mult)
                ve.tensor_scalar(Zbd, blocks, ps[:, 7, P:P + 1], None, ALU.mult).then_inc(la_bd, 1)
                for cc in range(CPB):
                    c = b * CPB + cc
                    dve.wait_ge(la_den, c + 2)
                    ve.tensor_scalar(rden, ps[:, 4, :], LA_EPS, None, ALU.add).then_inc(la_rden, 1)
                    dve.wait_ge(la_rden, 2 * c + 2)
                    ve.reciprocal(rden, rden).then_inc(la_rden, 1)
                    dve.wait_ge(la_rden, 2 * c + 3)
                    ve.tensor_tensor(att, ps[:, 3, :], rden, ALU.mult).then_inc(la_att, 1)
                    n = b * 6 + 2 + 2 * cc
                    ln_a(n)
                    ln_b(n, xn[:, 1, :])
                    dve.wait_ge(ln_out, n + 2)
                    ve.tensor_tensor(x1[:, bass.ds(c * CH, CH)], x1[:, bass.ds(c * CH, CH)], xn[:, 1, :],
                                     ALU.add).then_inc(la_x1, 1)
                    ln_a(n + 1)
                    ln_b(n + 1, xin[:, bass.ds(ccol(c), CH)])

            def shift(dst, src, col, width):
                ve.tensor_copy(dst[0:64, :], src[0:64, bass.ds(col, width)])
                return ve.tensor_copy(dst[64:P, :], src[64:P, bass.ds(col - 1, width)])

            def products(l, t, h):
                dve.wait_ge(sq_done[h], l * TILES + t + 2)
                dve.wait_ge(tk_done[h], l * TILES + t + 1)
                tt = t % TPB
                tab = rot_tab[:, bass.ds(tt, 1), :, :].rearrange("p a s n -> p (a s) n")
                qk = ps[:, 0:2, :].rearrange("p a (h d) -> p a h d", d=HD)
                ve.tensor_tensor(rotA[:, h, :].rearrange("p (a h d) -> p a h d", a=2, d=HD), qk,
                                 tab[:, 0, :].rearrange("p (a d) -> p a d", a=2).unsqueeze(2).broadcast_to([P, 2, 8, HD]),
                                 ALU.mult)
                swapped = ps[:, 0:2, :].rearrange("p a (h x f) -> p (a h) x f", x=2, f=32)[:, :, ::-1, :]
                ve.tensor_tensor(rotB[:, h, :].rearrange("p (a h d) -> p a h d", a=2, d=HD), swapped,
                                 tab[:, 1, :].rearrange("p (a d) -> p a d", a=2).unsqueeze(2).broadcast_to([P, 2, 8, HD]),
                                 ALU.mult).then_inc(prod_done[h], 1)
                ve.tensor_reduce(nrm[:, h, :], sq[:, h, :].rearrange("p (a d) -> p a d", d=HD), AX.X,
                                 ALU.add).then_inc(nrm_done[h], 1)
                dve.wait_ge(nrm_done[h], l * TILES + t + 2)
                dve.wait_ge(r_done[h], l * TILES + t + 1)
                ve.tensor_scalar(nsq[:, h, :], nrm[:, h, :], L2_EPS * L2_EPS, None, ALU.max).then_inc(nsq_done[h], 1)

            def slot(l, t, p, qk, mid, av, more):
                if qk:
                    products(l, t, 0)
                if av:
                    dve.wait_ge(exp_done, l * TILES + t)
                    ve.tensor_reduce(ssum[:], prob[:], AX.X, ALU.add).then_inc(sum_done, 1)
                    dve.wait_ge(sum_done, l * TILES + t)
                    ve.reciprocal(rsum[:], ssum[:]).then_inc(rs_done, 1)
                if qk:
                    products(l, t, 1)
                if more:
                    dve.wait_ge(qk_done[1], l * TILES + t + 1)
                    shift(xs[:, 1 - p, :], xin, tcol(t + 1), P).then_inc(xs_done, 1)
                if mid:
                    if not (isinstance(t, int) and t < 3):
                        dve.wait_ge(v_done[1], l * TILES + t - 1)
                    shift(xsv[:, 1 - p, :], xin, tcol(t - 1), P).then_inc(xsv_done, 1)
                if av:
                    dve.wait_ge(norm_done, l * TILES + t)
                    dve.wait_ge(av_done[1], l * TILES + t - 1)
                    for w in range(NW):
                        q0 = WIN * w
                        ve.transpose(PT[q0:q0 + WIN, :, q0:q0 + WIN], prob[q0:q0 + WIN, :, WIN:])
                        if w:
                            last = ve.transpose(PT[q0 - WIN:q0, :, q0:q0 + WIN], prob[q0:q0 + WIN, :, 0:WIN])
                        else:
                            ve.transpose(PTp[P - WIN:P, :, :], prob[0:WIN, :, 0:WIN])
                    last.then_inc(pt_done, 1)
                if mid:
                    dve.wait_ge(s_done, l * TILES + t + 1)
                    dve.wait_ge(r_done[1], l * TILES + t + 1)
                    if av:
                        dve.wait_ge(pt_done, l * TILES + t)
                    ve.tensor_tensor(prob[:].rearrange("p (e a) n -> p e a n", e=2),
                                     ps[:, 4:6, :].rearrange("p e (a n) -> p e a n", n=2 * WIN),
                                     rq[:, 1 - p, :].rearrange("p (a e) -> p e a", e=2).unsqueeze(3)
                                     .broadcast_to([P, 2, PAIRS, 2 * WIN]), ALU.mult).then_inc(scaled, 1)
                    dve.wait_ge(scaled, l * TILES + t + 1)
                    ve.tensor_reduce(mx[:], prob[:], AX.X, ALU.max).then_inc(mx_done, 1)
                if av:
                    dve.wait_ge(y_done, l * TILES + t)
                    col = tcol(t - 2)
                    ve.tensor_tensor(xmid[:, bass.ds(col, P)], ps[:, 2, 0:P], xin[:, bass.ds(col, P)],
                                     ALU.add).then_inc(xmid_done, 1)

            with dve.Fori(0, DEPTH) as l:
                dve.wait_ge(xout_done, l * CHUNKS + 1)
                dve.wait_ge(ln_out, LN_PRE + l * CHUNKS + 1)
                dve.wait_ge(tab_done, l + 2)
                shift(xs[:, 0, :], xin, tcol(0), P).then_inc(xs_done, 1)
                slot(l, 0, 0, True, False, False, True)
                slot(l, 1, 1, True, True, False, True)
                with dve.Fori(0, TILES // 2 - 2) as j:
                    for p in range(2):
                        slot(l, 2 * j + 2 + p, p, True, True, True, True)
                slot(l, TILES - 2, 0, True, True, True, True)
                slot(l, TILES - 1, 1, True, True, True, False)
                slot(l, TILES, 0, False, True, True, False)
                slot(l, TILES + 1, 1, False, False, True, False)
                dve.wait_ge(s_wffn, l * N_WFFN + N_WFFN)
                dve.wait_ge(xmid_done, l * TILES + TILES + 1)
                n = LN_PRE + l * CHUNKS
                shift(xsf, xmid, ccol(0), CH).then_inc(xsf_done, 1)
                ln_a(n)
                ln_b(n, xn[:, 0, :], True)
                for c in range(CHUNKS):
                    more = c + 1 < CHUNKS
                    if more:
                        dve.wait_ge(ln_cen, n + c + 2)
                        shift(xsf, xmid, ccol(c + 1), CH).then_inc(xsf_done, 1)
                    for m, (_, fb) in enumerate(FBLK):
                        k = 3 * c + m
                        dve.wait_ge(gl_done, l * 12 + k + 2)
                        if m == 0:
                            dve.wait_ge(f_done, l * CHUNKS + c + 1)
                        ve.scalar_tensor_tensor(hm[0:fb, m, :], ps[0:fb, 3 + k % 2, :], b1a[0:fb, m:m + 1],
                                                gl[0:fb, k % 2, :], ALU.add, ALU.mult).then_inc(hm_done, 1)
                        if more and m == 0:
                            ln_a(n + c + 1)
                        if more and m == 1:
                            ln_b(n + c + 1, xn[:, (c + 1) % 2, :], True)
                    dve.wait_ge(f_done, l * CHUNKS + c + 2)
                    col = ccol(c)
                    ve.scalar_tensor_tensor(xin[:, col:col + CH], ps[:, 7, :], b2c[:], xmid[:, col:col + CH],
                                            ALU.add, ALU.add).then_inc(xout_done, 1)

            with dve.Fori(0, CHUNKS) as c:
                ln_a(LN_FIN + c)
                dve.wait_ge(fin_T, c + 1)
                ln_b(LN_FIN + c, xn[:, 0, :])
                dve.wait_ge(ln_out, LN_FIN + c + 2)
                ve.tensor_tensor(xn[:, 0, :], xn[:, 0, :], x1[:, bass.ds(c * CH, CH)], ALU.add).then_inc(fin_add, 1)
                dve.wait_ge(fin_T, c + 2)
                dve.wait_ge(s_out, 16 * c + 16)
                ve.tensor_copy(ost, ps[:, 3, :].rearrange("p (i f) -> p i f", i=4)).then_inc(fin_copied, 1)

        @block.tensor
        def _(pe):
            te = nc.tensor

            def mm(o, lhsT, rhs, start=True, stop=True, **kw):
                return te.matmul(o, lhsT, rhs, start=start, stop=stop, **kw)

            def tr(o, i):
                return te.matmul(o, i, ident, start=True, stop=True, is_transpose=True)

            def ln_a(n, src):
                mm(ps[:, 0, :], centre, src).then_inc(ln_cen, 1)

            def ln_b(n):
                pe.wait_ge(ln_sq, n + 2)
                for i in range(4):
                    ins = mm(ps[:, 1, i:i + 1], ln_sqb[:, i * P:(i + 1) * P], ones_m[:, 0:1])
                ins.then_inc(ln_var, 1)

            def ln_c(n):
                pe.wait_ge(ln_pow, n + 2)
                pe.wait_ge(ln_out, n + 1)
                for i in range(4):
                    ins = tr(ps[:, 2, i * P:(i + 1) * P], ln_r[:, i:i + 1].broadcast_to([P, P]))
                ins.then_inc(ln_bc, 1)

            pe.wait_ge(s_const, 48)
            pe.wait_ge(s_wla, 64)
            for i in range(4):
                ins = tr(ps[:, 3, i * P:(i + 1) * P], wnat[:, i, :])
            ins.then_inc(wT_done, 1)
            pe.wait_ge(wT_copied, 1)
            with pe.Fori(0, B) as b:
                for cc in range(CPB):
                    c = b * CPB + cc
                    n = b * 6 + cc
                    pe.wait_ge(s_x, 16 * c + 16)
                    pe.wait_ge(la_att, b * CPB + 1)
                    for i in range(4):
                        ins = tr(ps[:, 3, i * P:(i + 1) * P], xst[:, i, :])
                    ins.then_inc(xT_done, 1)
                    pe.wait_ge(xT_copied, c + 2)
                    ln_a(n, x1[:, bass.ds(c * CH, CH)])
                    ln_b(n)
                    ln_c(n)
                    pe.wait_ge(ln_out, n + 2)
                    mm(ps[:, 4, :], wT[:, 0, :], xn[:, 0, :]).then_inc(la_q, 1)
                    for i in range(4):
                        ins = mm(ps[:, 5 + i // 2, (i % 2) * 256:(i % 2) * 256 + 256], xn[:, 0, i * P:(i + 1) * P],
                                 wT[:, 1:3, :].rearrange("p a n -> p (a n)"))
                    ins.then_inc(la_kv, 1)
                    pe.wait_ge(la_phik, c + 2)
                    for i in range(4):
                        ins = mm(ps[:, 7, 0:P + 1], phiK[:, i * P:(i + 1) * P], Vo[:, i, 0:P + 1],
                                 start=(cc == 0 and i == 0), stop=(cc == CPB - 1 and i == 3))
                    if cc == CPB - 1:
                        ins.then_inc(la_sum, 1)
                pe.wait_ge(la_bd, b + 2)
                for cc in range(CPB):
                    c = b * CPB + cc
                    n = b * 6 + 2 + 2 * cc
                    pe.wait_ge(la_att, c + 1)
                    mm(ps[:, 3, :], KVbd, phiQ[:, cc, :]).then_inc(la_num, 1)
                    mm(ps[:, 4, :], Zbd, phiQ[:, cc, :]).then_inc(la_den, 1)
                    pe.wait_ge(la_att, c + 2)
                    mm(ps[:, 5, :], wT[:, 3, :], att).then_inc(la_y, 1)
                    pe.wait_ge(la_ysb, c + 2)
                    ln_a(n, ysb)
                    ln_b(n)
                    ln_c(n)
                    pe.wait_ge(la_x1, c + 2)
                    ln_a(n + 1, x1[:, bass.ds(c * CH, CH)])
                    ln_b(n + 1)
                    ln_c(n + 1)

            def qk(l, t, p, h):
                if h == 0:
                    pe.wait_ge(xs_done, l * TILES + t + 2)
                pe.wait_ge(prod_done[1 - h], l * TILES + t + h + 1)
                pe.wait_ge(sq_done[1 - h], l * TILES + t + h + 1)
                for a in range(2):
                    o = a * INNER + h * HALF
                    ins = mm(ps[:, a, :], xs[:, p, :], wqkv[:, o:o + HALF])
                ins.then_inc(qk_done[h], 1)

            def tq(l, t, h):
                pe.wait_ge(add_done[h], l * TILES + t + 2)
                pe.wait_ge(tk_evac[1 - h], l * TILES + t + h + 1)
                for i in range(4):
                    ins = tr(ps[:, 3, i * P:(i + 1) * P], rotA[:, h, i * P:(i + 1) * P])
                ins.then_inc(tq_done[h], 1)

            def tk(l, t, h):
                pe.wait_ge(kmul_done[h], l * TILES + t + 2)
                pe.wait_ge(tq_evac[h], l * TILES + t + 2)
                for i in range(4):
                    ins = tr(ps[:, 3, i * P:(i + 1) * P], rotA[:, h, HALF + i * P:HALF + (i + 1) * P])
                ins.then_inc(tk_done[h], 1)

            def v(l, t, p, h):
                if h == 0:
                    pe.wait_ge(xsv_done, l * TILES + t + 2)
                    pe.wait_ge(xmid_done, l * TILES + t + 1)
                else:
                    pe.wait_ge(v_evac[0], l * TILES + t + 2)
                o = 2 * INNER + h * HALF
                mm(ps[:, 2, :], xsv[:, p, :], wqkv[:, o:o + HALF]).then_inc(v_done[h], 1)

            def scores(l, t):
                pe.wait_ge(tk_evac[1], l * TILES + t + 2)
                pe.wait_ge(scaled, l * TILES + t + 1)
                for e in range(2):
                    mm(ps[:, 4 + e, :], ident_b[:], mask[:, bass.ds(t, 1), :].broadcast_to([P, PAIRS, 2 * WIN]),
                       stop=False, skip_group_check=True)
                for a in range(PAIRS):
                    for w in range(NW):
                        for e in range(2):
                            last = a == PAIRS - 1 and w == NW - 1 and e == 1
                            ins = mm(ps[WIN * w:WIN * w + WIN, 4 + e, a * 64:a * 64 + 64],
                                     qT[64 * e:64 * e + 64, a, WIN * w:WIN * w + WIN],
                                     kT[64 * e:64 * e + 64, a, WIN * w:WIN * w + 2 * WIN],
                                     start=False, stop=True, skip_group_check=True)
                ins.then_inc(s_done, 1)

            def av(l, t, p, h):
                pe.wait_ge(v_evac[1], l * TILES + t + 2)
                pe.wait_ge(o_evac[h], l * TILES + t + 1)
                pe.wait_ge(pt_done, l * TILES + t + 2)
                for i in range(4):
                    for e in range(2):
                        a = 4 * h + i
                        o = (2 * a + e) * HD
                        dst = ps[64 * e:64 * e + 64, 6 + h, i * P:(i + 1) * P]
                        mm(dst, V[:, p, o:o + HD], PT[:, e * PAIRS + a, :], stop=False, skip_group_check=True)
                        ins = mm(dst[:, 0:WIN], V[P - WIN:P, 1 - p, o:o + HD], PTp[P - WIN:P, e * PAIRS + a, :],
                                 start=False, skip_group_check=True)
                ins.then_inc(av_done[h], 1)

            def project(l, t):
                pe.wait_ge(o_evac[0], l * TILES + t + 2)
                pe.wait_ge(o_evac[1], l * TILES + t + 2)
                for a in range(PAIRS):
                    ins = mm(ps[:, 2, 0:P], wo[:, a, :], oT[:, a, :], start=(a == 0), stop=(a == PAIRS - 1))
                ins.then_inc(y_done, 1)

            def slot(l, t, p, has_qk, mid, has_av):
                if has_qk:
                    qk(l, t, p, 0)
                if mid:
                    tq(l, t - 1, 1)
                if has_av:
                    v(l, t - 2, p, 0)
                if mid:
                    tk(l, t - 1, 1)
                if has_av:
                    v(l, t - 2, p, 1)
                if has_qk:
                    qk(l, t, p, 1)
                if mid:
                    scores(l, t - 1)
                if has_qk:
                    tq(l, t, 0)
                if has_av:
                    av(l, t - 2, p, 0)
                if has_qk:
                    tk(l, t, 0)
                if has_av:
                    av(l, t - 2, p, 1)
                    project(l, t - 2)

            pe.wait_ge(init_v, 4)
            pe.wait_ge(init_p, 4)
            with pe.Fori(0, DEPTH) as l:
                pe.wait_ge(s_wattn, l * N_WATTN + N_WATTN)
                slot(l, 0, 0, True, False, False)
                slot(l, 1, 1, True, True, False)
                with pe.Fori(0, TILES // 2 - 1) as j:
                    for p in range(2):
                        slot(l, 2 * j + 2 + p, p, True, True, True)
                slot(l, TILES, 0, False, True, True)
                slot(l, TILES + 1, 1, False, False, True)
                pe.wait_ge(s_wffn, l * N_WFFN + N_WFFN)
                n = LN_PRE + l * CHUNKS
                pe.wait_ge(xsf_done, l * CHUNKS + 2)
                ln_a(n, xsf[:])
                ln_b(n)
                ln_c(n)
                for c in range(CHUNKS):
                    more = c + 1 < CHUNKS
                    if more:
                        pe.wait_ge(xsf_done, l * CHUNKS + c + 3)
                        ln_a(n + c + 1, xsf[:])
                    pe.wait_ge(ln_out, n + c + 2)
                    for m, (o, fb) in enumerate(FBLK):
                        k = 3 * c + m
                        if k >= 2:
                            pe.wait_ge(hm_done, l * 12 + k)
                        mm(ps[0:fb, 3 + k % 2, :], w1[:, o:o + fb], xn[:, c % 2, :])
                        mm(ps[0:fb, 5 + k % 2, :], w1[:, FF + o:FF + o + fb], xn[:, c % 2, :]).then_inc(h_done, 1)
                        if more and m == 0:
                            ln_b(n + c + 1)
                        if more and m == 1:
                            ln_c(n + c + 1)
                    if c:
                        pe.wait_ge(xout_done, l * CHUNKS + c + 1)
                    pe.wait_ge(hm_done, l * 12 + 3 * c + 4)
                    for m, (o, fb) in enumerate(FBLK):
                        ins = mm(ps[:, 7, :], w2[0:fb, m, :], hm[0:fb, m, :], start=(m == 0), stop=(m == 2))
                    ins.then_inc(f_done, 1)

            pe.wait_ge(xout_done, DEPTH * CHUNKS + 1)
            with pe.Fori(0, CHUNKS) as c:
                ln_a(LN_FIN + c, xin[:, bass.ds(ccol(c), CH)])
                ln_b(LN_FIN + c)
                ln_c(LN_FIN + c)
                pe.wait_ge(fin_add, c + 2)
                pe.wait_ge(fin_copied, c + 1)
                for i in range(4):
                    ins = tr(ps[:, 3, i * P:(i + 1) * P], xn[:, 0, i * P:(i + 1) * P])
                ins.then_inc(fin_T, 1)


_INS = ['L0_attn_x', 'L0_attn_Wq', 'L0_attn_bq', 'L0_attn_Wk', 'L0_attn_bk', 'L0_attn_Wv', 'L0_attn_bv',
        'L0_attn_Wo', 'L0_attn_bo', 'L0_ffn_Wqkv', 'L0_ffn_q_scale', 'L0_ffn_k_scale', 'L0_ffn_Wo',
        'L0_ffn_ln_g', 'L0_ffn_ln_b', 'L0_ffn_W1', 'L0_ffn_b1', 'L0_ffn_W2', 'L0_ffn_b2']


def _constants():
    import numpy as np

    i = np.arange(P)
    mats = np.stack([np.eye(P), np.eye(P) - 1.0 / P, (i[:, None] // LA_HD == i[None, :] // LA_HD),
                     np.full((P, P), 1.0 / P)], 1).astype(np.float32)
    half = np.arange(0, HD, 2, dtype=np.float32)
    inv_freq = (np.float32(1.0) / np.float32(10000.0) ** (half / np.float32(HD))).astype(np.float32)
    pos = np.arange(N, dtype=np.float32)
    freqs = pos[:, None] * inv_freq[None, :]
    base = (half + np.float32(0.4 * HD)) / np.float32(1.4 * HD)
    power = (pos - N // 2) / np.float32(WIN // 2)
    scale = (base[None, :] ** power[:, None]).astype(np.float32)
    cos, sin = np.cos(freqs), np.sin(freqs)
    both = []
    for s in (scale, np.float32(1.0) / scale):
        both.append((np.concatenate([cos * s, cos * s], 1), np.concatenate([-sin * s, sin * s], 1)))
    rot = np.stack([np.concatenate([both[0][k], both[1][k]], 1) for k in range(2)], 1)
    rot = rot.reshape(TPB, P, 2, P).transpose(1, 0, 2, 3).astype(np.float32)
    q, j = np.arange(P)[:, None] % WIN, np.arange(2 * WIN)[None, :]
    seen = (j >= q) & (j <= q + WIN)
    first = seen & ~((np.arange(P)[:, None] < WIN) & (j < WIN))
    mask = np.where(np.stack([first, seen], 1), 0.0, -1e30).astype(np.float32)
    return {"c_mats": mats, "c_rot": rot, "c_mask": mask}


def kernel(**inputs):
    import numpy as np
    import concourse.bacc as bacc
    from concourse.bass_utils import run_bass_kernel_spmd

    nc = bacc.Bacc("TRN2", target_bir_lowering=False, num_devices=1)
    arrays, args = {}, []
    given = {name: np.ascontiguousarray(inputs[name]) for name in _INS}
    given.update({k: np.ascontiguousarray(a) for k, a in _constants().items()})
    for name, a in given.items():
        arrays[f"in_{name}"] = a
        args.append(nc.dram_tensor(f"in_{name}", a.shape, mybir.dt.from_np(a.dtype), kind="ExternalInput").ap())
    o = nc.dram_tensor("out_0", (B, N, P), F32, kind="ExternalOutput").ap()
    program(nc, *args, o)
    r = run_bass_kernel_spmd(nc, [arrays], core_ids=[0])
    return r.results[0]["out_0"]
```

```python
import concourse.bass as bass
from concourse import mybir
from concourse.alu_op_type import AluOpType as ALU
from contextlib import ExitStack

F32 = mybir.dt.float32
BF16 = mybir.dt.bfloat16
I32 = mybir.dt.int32
ACT = mybir.ActivationFunctionType
AX = mybir.AxisListType

P = 128
B, N = 2, 1024
TOK = B * N
TILES = TOK // P
TPB = TILES // B
CH = 512
CHUNKS = TOK // CH
CPB = CHUNKS // B
DEPTH, HEADS, HD, WIN = 6, 16, 64, 32
INNER = HEADS * HD
PAIRS = HEADS // 2
HALF = INNER // 2
FF = 341
FB = 114
FBLK = [(0, 114), (114, 114), (228, 113)]
NW = P // WIN
LA_HD = 8
LA_EPS, LN_EPS, L2_EPS = 1e-6, 1e-5, 1e-12
RSQRT_BITS = 1597463007.0
TQ_BANK, TK_BANK, V_BANK, O_BANK, Y_BANK = (6, 3), (3, 6), (7, 3), (7, 6), 2
LN_PRE = 3 * CHUNKS
LN_FIN = LN_PRE + CHUNKS * DEPTH


def tcol(t):
    return t * P + t // TPB + 1


def ccol(c):
    return c * CH + c // CPB + 1


def program(nc, x, Wq, bq, Wk, bk, Wv, bv, Wo, bo, Wqkv, q_scale, k_scale, Wo6, ln_g, ln_b,
            W1, b1, W2, b2, c_mats, c_rot, c_mask, out):
    ctx = ExitStack()
    with ctx:
        def sb(name, shape, dt=F32):
            return ctx.enter_context(nc.sbuf_tensor(name, shape, dt))

        def sem(name):
            return ctx.enter_context(nc.semaphore(name))

        seeded = []

        def cnt(name):
            seeded.append(sem(name))
            return seeded[-1]

        def cnt2(name):
            return [cnt(f"{name}{i}") for i in range(2)]

        mats = sb("mats", [P, 4, P])
        ident, centre, blocks, ones_m = (mats[:, i, :] for i in range(4))
        ident_b = sb("ident_b", [P, P], BF16)
        mask_f = sb("mask_f", [P, 2, HD])
        mask = sb("mask", [P, TILES, HD], BF16)
        keep = sb("keep", [P, TILES + 1])
        minus_half = sb("minus_half", [P, 4])
        one_half = sb("one_half", [P, 2, HEADS])
        newt_z = sb("newt_z", [P, 2, HEADS])
        newt_u = sb("newt_u", [P, 2, HEADS])
        rot_base = sb("rot_base", [P, TPB, 2, P])
        rot_tab = sb("rot_tab", [P, TPB, 2, P])
        scales = sb("scales", [P, 2, P])
        x1 = sb("x1", [P, TOK])
        xin = sb("xin", [P, TOK + B + 2])
        xmid = sb("xmid", [P, TOK + B + 2])
        wqkv = sb("wqkv", [P, 3 * INNER])
        wo = sb("wo", [P, PAIRS, P])
        w1 = sb("w1", [P, 2 * FF])
        w2 = sb("w2", [FB, 3, P])
        lng = sb("lng", [P, 1])
        lnb = sb("lnb", [P, 1])
        b1a = sb("b1a", [FB, 3])
        b1g = sb("b1g", [FB, 3])
        b2c = sb("b2c", [P, 1])
        xs = sb("xs", [P, 2, P])
        xsv = sb("xsv", [P, 2, P])
        sq = sb("sq", [P, 2, 2 * HALF])
        rotA = sb("rotA", [P, 2, 2, 2 * HALF])
        rotB = sb("rotB", [P, 2, 2 * HALF])
        nsq = sb("nsq", [P, 2, HEADS])
        nrm = sb("nrm", [P, 2, HEADS])
        nhalf = sb("nhalf", [P, 2, HEADS])
        rinv = sb("rinv", [P, 2, HEADS])
        rq = sb("rq", [P, 2, 2, 8])
        qT = sb("qT", [P, PAIRS, P])
        kT = sb("kT", [P, PAIRS, WIN + P])
        V = sb("V", [P, 2, INNER])
        prob = sb("prob", [P, 2, HEADS, 2 * WIN])
        mx = sb("mx", [P, HEADS])
        mxn = sb("mxn", [P, HEADS])
        ssum = sb("ssum", [P, HEADS])
        rsum = sb("rsum", [P, HEADS])
        PT = sb("PT", [P, 2, HEADS, P])
        PTp = sb("PTp", [P, 2, HEADS, 2 * WIN])
        oT = sb("oT", [P, PAIRS, P])
        ln_sqb = sb("ln_sqb", [P, CH])
        ln_xcb = sb("ln_xcb", [P, CH])
        ln_ve = sb("ln_ve", [P, 4])
        ln_r = sb("ln_r", [P, 4])
        xsf = sb("xsf", [P, CH])
        xn = sb("xn", [P, 2, CH])
        gl = sb("gl", [FB, 2, CH])
        hm = sb("hm", [FB, 3, CH])
        ps = ctx.enter_context(nc.psum_tensor("ps", [P, 8, CH], F32))

        wnat = rotB[:, 0, 0:512].rearrange("p (a n) -> p a n", a=4)
        wT = rotB[:, 0, 512:1024].rearrange("p (a n) -> p a n", a=4)
        bq_c, bo_c = rsum[:, 0:1], rsum[:, 1:2]
        bkv = sb("bkv", [P, 2, P])
        xst = sq[:, 0, 0:512].rearrange("p (i f) -> p i f", i=4)
        phiQ = wqkv[:, 0:2 * CH].rearrange("p (c n) -> p c n", c=2)
        relu_t = sq[:, 1, 0:512]
        min_t = sq[:, 1, 512:1024]
        kz = rotA[:, 0, 0, 0:512]
        phiK = rotA[:, 0, 0, 512:1024]
        Vo = wqkv[:, 1024:1024 + 4 * 130].rearrange("p (i n) -> p i n", i=4)
        KVbd = rotA[:, 0, 1, 0:128]
        Zbd = rotA[:, 0, 1, 128:256]
        rden = rotA[:, 0, 1, 512:1024]
        att = rotB[:, 1, 0:512]
        ysb = rotB[:, 1, 512:1024]
        ost = sq[:, 0, 512:1024].rearrange("p (i f) -> p i f", i=4)

        s_const, s_bias, s_wla, s_x, s_out = map(sem, ["s_const", "s_bias", "s_wla", "s_x", "s_out"])
        s_wattn, s_wffn = sem("s_wattn"), sem("s_wffn")
        s_init = sem("s_init")
        init_v, init_p = sem("init_v"), sem("init_p")
        wT_done, wT_copied = sem("wT_done"), sem("wT_copied")
        xT_done, xT_copied = cnt("xT_done"), cnt("xT_copied")
        ln_cen, ln_sq, ln_var, ln_eps, ln_pow, ln_bc, ln_mul, ln_out = map(
            cnt, ["ln_cen", "ln_sq", "ln_var", "ln_eps", "ln_pow", "ln_bc", "ln_mul", "ln_out"])
        la_q, la_qmin, la_qexp, la_phiq = map(cnt, ["la_q", "la_qmin", "la_qexp", "la_phiq"])
        la_kv, la_kb, la_kmin, la_kexp, la_phik = map(cnt, ["la_kv", "la_kb", "la_kmin", "la_kexp", "la_phik"])
        la_sum, la_bd, la_num, la_den, la_rden, la_att, la_y, la_ysb, la_x1 = map(
            cnt, ["la_sum", "la_bd", "la_num", "la_den", "la_rden", "la_att", "la_y", "la_ysb", "la_x1"])
        tab_done = cnt("tab_done")
        xs_done, xsv_done = cnt("xs_done"), cnt("xsv_done")
        qk_done, sq_done, prod_done = map(cnt2, ["qk_done", "sq_done", "prod_done"])
        nsq_done = cnt("nsq_done")
        add_done = cnt2("add_done")
        kmul_done, r_done, guess_done, newton, newton_y = map(cnt, ["kmul_done", "r_done", "guess_done", "newton", "newton_y"])
        nrm_done = cnt2("nrm_done")
        tq_done, tq_evac, tk_done, tk_evac = map(cnt2, ["tq_done", "tq_evac", "tk_done", "tk_evac"])
        kprev = cnt("kprev")
        v_done, v_evac, av_done, o_evac = map(cnt2, ["v_done", "v_evac", "av_done", "o_evac"])
        s_done, mx_done, mxn_done, exp_done, sum_done, rs_done, norm_done, pt_done, y_done, xmid_done = map(
            cnt, ["s_done", "mx_done", "mxn_done", "exp_done", "sum_done", "rs_done", "norm_done",
                  "pt_done", "y_done", "xmid_done"])
        xsf_done, h_done, gl_done, hm_done, f_done, xout_done = map(
            cnt, ["xsf_done", "h_done", "gl_done", "hm_done", "f_done", "xout_done"])
        fin_add, fin_T, fin_copied = map(cnt, ["fin_add", "fin_T", "fin_copied"])

        block = ctx.enter_context(nc.Block())

        @block.sync
        def _(sp):
            for counter in seeded:
                sp.sem_inc(counter, 1)
            sp.dma_start(mats[:], c_mats).then_inc(s_const, 16)
            sp.dma_start(wnat[:, 0, :], Wq).then_inc(s_wla, 16)
            sp.dma_start(wnat[:, 1, :], Wk).then_inc(s_wla, 16)
            sp.dma_start(wnat[:, 2, :], Wv).then_inc(s_wla, 16)
            sp.dma_start(wnat[:, 3, :], Wo).then_inc(s_wla, 16)
            sp.dma_start(mask_f[:], c_mask).then_inc(s_const, 16)
            sp.dma_start(rot_base[:], c_rot).then_inc(s_const, 16)
            sp.dma_start(bq_c, bq.rearrange("(p a) -> p a", a=1)).then_inc(s_bias, 16)
            sp.dma_start(bo_c, bo.rearrange("(p a) -> p a", a=1)).then_inc(s_bias, 16)
            sp.dma_start(bkv[:, 0, :], bk.partition_broadcast(P)).then_inc(s_bias, 16)
            sp.dma_start(bkv[:, 1, :], bv.partition_broadcast(P)).then_inc(s_bias, 16)
            xr = x.rearrange("b (c i p) f -> (b c) p i f", i=4, p=P)
            with sp.Fori(0, CHUNKS) as c:
                sp.wait_ge(xT_done, c + 1)
                sp.dma_start(xst, xr[bass.ds(c, 1), :, :, :].rearrange("a p i f -> (a p) i f")).then_inc(s_x, 16)
            sp.wait_ge(la_x1, CHUNKS + 1)
            with sp.Fori(0, DEPTH) as l:
                sp.wait_ge(v_done[1], l * TILES + 1)
                sp.dma_start(wqkv[:], Wqkv[bass.ds(l, 1), :, :].rearrange("a p n -> (a p) n")).then_inc(s_wattn, 16)
                sp.wait_ge(tab_done, l + 1)
                for qk, s in ((0, q_scale), (1, k_scale)):
                    row = s[bass.ds(l, 1), :].rearrange("a d -> (a d)")
                    o = qk * HD
                    sp.dma_start(scales[:, 0, o:o + HD], row.partition_broadcast(P)).then_inc(s_wattn, 16)
                    sp.dma_start(scales[:, 1, o:o + 32], row[32:64].partition_broadcast(P)).then_inc(s_wattn, 16)
                    sp.dma_start(scales[:, 1, o + 32:o + 64], row[0:32].partition_broadcast(P)).then_inc(s_wattn, 16)
                sp.wait_ge(y_done, l * TILES + 1)
                sp.dma_start(wo[:], Wo6[bass.ds(l, 1), :, :].rearrange("a (k p) n -> (a p) k n", p=P)).then_inc(s_wattn, 16)
                sp.wait_ge(xout_done, l * CHUNKS + 1)
                sp.dma_start(w1[:], W1[bass.ds(l, 1), :, :].rearrange("a p n -> (a p) n")).then_inc(s_wffn, 16)
                w2l = W2[bass.ds(l, 1), :, :].rearrange("a k n -> (a k) n")
                b1l = b1[bass.ds(l, 1), :].rearrange("a n -> (a n)")
                sp.dma_start(w2[:, 0:2, :], w2l[0:228, :].rearrange("(m k) n -> k m n", m=2)).then_inc(s_wffn, 16)
                sp.dma_start(w2[0:113, 2, :], w2l[228:341, :]).then_inc(s_wffn, 16)
                for dst, o in ((b1a, 0), (b1g, FF)):
                    sp.dma_start(dst[:, 0:2], b1l[o:o + 228].rearrange("(m k) -> k m", m=2),
                                 allow_slow_non_contiguous=True).then_inc(s_wffn, 16)
                    sp.dma_start(dst[0:113, 2:3], b1l[o + 228:o + 341].rearrange("(k a) -> k a", a=1)).then_inc(s_wffn, 16)
                for dst, src in ((lng, ln_g), (lnb, ln_b), (b2c, b2)):
                    sp.dma_start(dst[:], src[bass.ds(l, 1), :].rearrange("a (p q) -> (a p) q", q=1)).then_inc(s_wffn, 16)
            sp.sem_inc(s_out, 16)
            outr = out.rearrange("b (c i p) f -> (b c) p i f", i=4, p=P)
            with sp.Fori(0, CHUNKS) as c:
                sp.wait_ge(fin_copied, c + 2)
                sp.dma_start(outr[bass.ds(c, 1), :, :, :].rearrange("a p i f -> (a p) i f"), ost).then_inc(s_out, 16)
            sp.wait_ge(s_out, 16 * CHUNKS + 16)
        N_WATTN, N_WFFN = 8 * 16, 10 * 16

        @block.gpsimd
        def _(pool):
            gp = nc.gpsimd
            own = [0]

            gp.memset(minus_half[:], -0.5).then_inc(init_p, 1)
            gp.memset(one_half[:], 1.5)
            gp.memset(PTp[:], 0.0)
            gp.memset(PT[:], 0.0).then_inc(init_p, 1)
            gp.memset(kT[:], 0.0).then_inc(init_p, 1)
            gp.memset(V[:], 0.0).then_inc(init_p, 1)
            pool.wait_ge(init_p, 4)

            def ln(n):
                pool.wait_ge(ln_eps, n + 2)
                gp.tensor_tensor(ln_r[:], ln_ve[:], minus_half[:], ALU.pow).then_inc(ln_pow, 1)

            with pool.Fori(0, B) as b:
                for cc in range(CPB):
                    c = b * CPB + cc
                    ln(b * 6 + cc)
                    pool.wait_ge(la_qexp, c + 2)
                    gp.tensor_tensor(phiQ[:, cc, :], relu_t, min_t, ALU.add).then_inc(la_phiq, 1)
                    pool.wait_ge(la_kexp, c + 2)
                    gp.tensor_tensor(phiK, relu_t, min_t, ALU.add).then_inc(la_phik, 1)
                for cc in range(CPB):
                    ln(b * 6 + 2 + 2 * cc)
                    ln(b * 6 + 3 + 2 * cc)

            def add(l, t, p, h):
                pool.wait_ge(prod_done[h], l * TILES + t + 2)
                gp.tensor_tensor(rotA[:, p, h, :], rotA[:, p, h, :], rotB[:, h, :], ALU.add).then_inc(add_done[h], 1)

            def newton_step(l, t, it):
                done = (l * TILES + t) * 9 + 3 * it + 1
                pool.wait_ge(newton_y, (l * TILES + t) * 3 + it + 1)
                gp.tensor_tensor(newt_z[:], rinv[:], rinv[:], ALU.mult).then_inc(newton, 1)
                pool.wait_ge(newton, done + 1)
                gp.tensor_tensor(newt_u[:], newt_z[:], nhalf[:], ALU.mult).then_inc(newton, 1)
                pool.wait_ge(newton, done + 2)
                gp.tensor_tensor(newt_z[:], newt_u[:], one_half[:], ALU.add).then_inc(newton, 1)
                pool.wait_ge(newton, done + 3)
                gp.tensor_tensor(rinv[:], newt_z[:], rinv[:], ALU.mult).then_inc(newton_y, 1)

            def scale_k(l, t, p):
                pool.wait_ge(newton_y, (l * TILES + t) * 3 + 4)
                kk = rotA[:, p, :, HALF:].rearrange("p h (a d) -> p h a d", d=HD)
                gp.tensor_tensor(kk, kk, rinv[:, :, 8:16].unsqueeze(3).broadcast_to([P, 2, 8, HD]),
                                 ALU.mult).then_inc(kmul_done, 1)
                gp.tensor_scalar(rq[:, p, :, :], rinv[:, :, 0:8], 8.0, None, ALU.mult).then_inc(r_done, 1)

            def normalise(l, t, p):
                pool.wait_ge(rs_done, l * TILES + t + 2)
                gp.tensor_tensor(prob[:, p], prob[:, p], rsum[:].unsqueeze(2).broadcast_to([P, HEADS, 2 * WIN]),
                                 ALU.mult).then_inc(norm_done, 1)

            def slot(l, s, p, qk, av):
                if qk:
                    add(l, s, p, 0)
                if av:
                    normalise(l, s - 2, p)
                if qk:
                    add(l, s, p, 1)
                    pool.wait_ge(guess_done, l * TILES + s + 2)
                    newton_step(l, s, 0)
                    newton_step(l, s, 1)
                    newton_step(l, s, 2)
                    scale_k(l, s, p)

            with pool.Fori(0, DEPTH) as l:
                pool.wait_ge(s_wattn, l * N_WATTN + N_WATTN)
                if True:
                    pool.wait_ge(s_const, 48)
                pool.wait_ge(prod_done[1], l * TILES + 1)
                for part in range(2):
                    ins = gp.tensor_tensor(rot_tab[:, :, part, :], rot_base[:, :, part, :],
                                           scales[:, part, :].unsqueeze(1).broadcast_to([P, TPB, P]), ALU.mult)
                ins.then_inc(tab_done, 1)
                slot(l, 0, 0, True, False)
                slot(l, 1, 1, True, False)
                with pool.Fori(0, TILES // 2 - 1) as j:
                    for p in range(2):
                        slot(l, 2 * j + 2 + p, p, True, True)
                slot(l, TILES, 0, False, True)
                slot(l, TILES + 1, 1, False, True)
                for c in range(CHUNKS):
                    ln(LN_PRE + l * CHUNKS + c)
            with pool.Fori(0, CHUNKS) as c:
                ln(LN_FIN + c)

        @block.scalar
        def _(act):
            ac = nc.scalar

            def ln(n):
                act.wait_ge(ln_cen, n + 2)
                act.wait_ge(ln_out, n + 1)
                ac.activation(ln_xcb[:], ps[:, 0, :], ACT.Copy)
                ac.activation(ln_sqb[:], ps[:, 0, :], ACT.Square).then_inc(ln_sq, 1)

            act.wait_ge(s_bias, 64)
            with act.Fori(0, B) as b:
                for cc in range(CPB):
                    c = b * CPB + cc
                    ln(b * 6 + cc)
                    act.wait_ge(la_q, c + 2)
                    act.wait_ge(la_phik, c + 1)
                    act.wait_ge(la_qmin, c + 2)
                    ac.activation(relu_t, ps[:, 4, :], ACT.Relu, bias=bq_c)
                    ac.activation(min_t, min_t, ACT.Exp).then_inc(la_qexp, 1)
                    act.wait_ge(la_phiq, c + 2)
                    act.wait_ge(la_kb, c + 2)
                    ac.activation(relu_t, kz, ACT.Relu)
                    act.wait_ge(la_kmin, c + 2)
                    ac.activation(min_t, min_t, ACT.Exp).then_inc(la_kexp, 1)
                for cc in range(CPB):
                    c = b * CPB + cc
                    act.wait_ge(la_y, c + 2)
                    act.wait_ge(ln_cen, b * 6 + 2 + 2 * cc + 1)
                    ac.activation(ysb, ps[:, 5, :], ACT.Identity, bias=bo_c).then_inc(la_ysb, 1)
                    ln(b * 6 + 2 + 2 * cc)
                    ln(b * 6 + 3 + 2 * cc)

            def sq_unit(l, t, h):
                act.wait_ge(qk_done[h], l * TILES + t + 2)
                act.wait_ge(nrm_done[h], l * TILES + t + 1)
                ac.activation(sq[:, h, :], ps[:, 0:2, :].rearrange("p a n -> p (a n)"), ACT.Square).then_inc(sq_done[h], 1)

            def evac_tq(l, t, h):
                act.wait_ge(tq_done[h], l * TILES + t + 2)
                act.wait_ge(s_done, l * TILES + t + 1)
                ac.activation(qT[:, 4 * h:4 * h + 4, :], ps[:, TQ_BANK[h], :].rearrange("p (a n) -> p a n", a=4),
                              ACT.Copy).then_inc(tq_evac[h], 1)

            def evac_tk(l, t, h):
                act.wait_ge(kprev, l * TILES + t + 1)
                act.wait_ge(tk_done[h], l * TILES + t + 2)
                ac.activation(kT[:, 4 * h:4 * h + 4, WIN:], ps[:, TK_BANK[h], :].rearrange("p (a n) -> p a n", a=4),
                              ACT.Copy).then_inc(tk_evac[h], 1)

            def evac_v(l, t, p, h):
                act.wait_ge(v_done[h], l * TILES + t + 2)
                act.wait_ge(av_done[1], l * TILES + t + 1)
                ac.activation(V[:, p, h * HALF:(h + 1) * HALF], ps[:, V_BANK[h], :], ACT.Copy).then_inc(v_evac[h], 1)

            def evac_o(l, t, h):
                act.wait_ge(av_done[h], l * TILES + t + 2)
                act.wait_ge(y_done, l * TILES + t + 1)
                ac.activation(oT[:, 4 * h:4 * h + 4, :], ps[:, O_BANK[h], :].rearrange("p (a n) -> p a n", a=4),
                              ACT.Copy).then_inc(o_evac[h], 1)

            def exps(l, t, p, e):
                if e == 0:
                    act.wait_ge(mxn_done, l * TILES + t + 2)
                for a in range(PAIRS):
                    hh, ae = a // 4, 2 * (a % 4) + e
                    i = e * PAIRS + a
                    ins = ac.activation(prob[:, p, i, :], ps[:, 4 + e, a * 64:a * 64 + 64], ACT.Exp,
                                        bias=mxn[:, i:i + 1], scale=rq[:, p, hh, ae:ae + 1])
                if e:
                    ins.then_inc(exp_done, 1)

            def keep_window(l, t):
                ac.activation(kT[:, :, 0:WIN], kT[:, :, P:P + WIN], ACT.Copy,
                              scale=keep[:, bass.ds(t + 1, 1)]).then_inc(kprev, 1)

            def copy_xs(l, t, p):
                act.wait_ge(xs_done, l * TILES + t + 2)
                if not (isinstance(t, int) and t < 2):
                    act.wait_ge(v_done[1], l * TILES + t)
                ac.activation(xsv[:, p, :], xs[:, p, :], ACT.Copy).then_inc(xsv_done, 1)

            def slot(l, s, p, score, av, o, qk=True, qk_next=True):
                if score:
                    copy_xs(l, s - 1, 1 - p)
                if o:
                    evac_o(l, s - 3, 0)
                if qk:
                    sq_unit(l, s, 1)
                if score:
                    evac_tk(l, s - 1, 0)
                    evac_tk(l, s - 1, 1)
                if o:
                    evac_o(l, s - 3, 1)
                if score:
                    exps(l, s - 1, 1 - p, 0)
                if av:
                    evac_v(l, s - 2, p, 0)
                    evac_v(l, s - 2, p, 1)
                if qk_next:
                    sq_unit(l, s + 1, 0)
                if score:
                    exps(l, s - 1, 1 - p, 1)
                    keep_window(l, s - 1)
                if qk:
                    evac_tq(l, s, 0)
                    evac_tq(l, s, 1)

            act.wait_ge(init_p, 4)
            act.wait_ge(init_v, 5)
            with act.Fori(0, DEPTH) as l:
                sq_unit(l, 0, 0)
                slot(l, 0, 0, False, False, False)
                slot(l, 1, 1, True, False, False)
                slot(l, 2, 0, True, True, False)
                with act.Fori(0, TILES // 2 - 2) as j:
                    for i in range(2):
                        slot(l, 2 * j + 3 + i, 1 - i, True, True, True)
                slot(l, TILES - 1, 1, True, True, True, True, False)
                slot(l, TILES, 0, True, True, True, False, False)
                slot(l, TILES + 1, 1, False, True, True, False, False)
                slot(l, TILES + 2, 0, False, False, True, False, False)
                act.wait_ge(s_wffn, l * N_WFFN + N_WFFN)
                ln(LN_PRE + l * CHUNKS)
                for c in range(CHUNKS):
                    if c + 1 < CHUNKS:
                        ln(LN_PRE + l * CHUNKS + c + 1)
                    for m, (_, fb) in enumerate(FBLK):
                        k = 3 * c + m
                        act.wait_ge(h_done, l * 12 + k + 2)
                        if k >= 2:
                            act.wait_ge(hm_done, l * 12 + k)
                        ac.activation(gl[0:fb, k % 2, :], ps[0:fb, 5 + k % 2, :], ACT.Gelu,
                                      bias=b1g[0:fb, m:m + 1]).then_inc(gl_done, 1)
            with act.Fori(0, CHUNKS) as c:
                ln(LN_FIN + c)

        @block.vector
        def _(dve):
            ve = nc.vector
            dve.wait_ge(s_const, 48)
            ve.tensor_copy(ident_b[:], ident)
            ve.tensor_copy(mask[:], mask_f[:, 1:2, :].broadcast_to([P, TILES, HD])).then_inc(init_v, 1)
            dve.wait_ge(init_v, 1)
            ve.tensor_copy(mask[:, 0:TILES:TPB, :], mask_f[:, 0:1, :].broadcast_to([P, B, HD])).then_inc(init_v, 1)
            ve.memset(keep[:], 1.0)
            ve.memset(xin[:], 0.0).then_inc(init_v, 1)
            ve.memset(xmid[:], 0.0).then_inc(init_v, 1)
            dve.wait_ge(init_v, 4)
            ve.memset(keep[:, 0:TILES + 1:TPB], 0.0).then_inc(init_v, 1)

            def ln_a(n):
                dve.wait_ge(ln_var, n + 2)
                ve.tensor_scalar(ln_ve[:], ps[:, 1, 0:4], LN_EPS, None, ALU.add).then_inc(ln_eps, 1)

            def ln_b(n, dst, affine=False):
                dve.wait_ge(ln_bc, n + 2)
                if not affine:
                    ve.tensor_tensor(dst, ps[:, 2, :], ln_xcb[:], ALU.mult).then_inc(ln_out, 1)
                else:
                    ve.tensor_tensor(dst, ps[:, 2, :], ln_xcb[:], ALU.mult).then_inc(ln_mul, 1)
                    dve.wait_ge(ln_mul, n - LN_PRE + 2)
                    ve.tensor_scalar(dst, dst, lng[:], lnb[:], ALU.mult, ALU.add).then_inc(ln_out, 1)

            dve.wait_ge(wT_done, 1)
            ve.tensor_copy(wT, ps[:, 3, :].rearrange("p (a n) -> p a n", a=4)).then_inc(wT_copied, 1)
            dve.wait_ge(s_bias, 64)
            ve.memset(Vo[:, :, P:P + 2], 1.0)
            with dve.Fori(0, B) as b:
                for cc in range(CPB):
                    c = b * CPB + cc
                    n = b * 6 + cc
                    dve.wait_ge(xT_done, c + 2)
                    ve.tensor_copy(x1[:, bass.ds(c * CH, CH)], ps[:, 3, :]).then_inc(xT_copied, 1)
                    ln_a(n)
                    ln_b(n, xn[:, 0, :])
                    dve.wait_ge(la_q, c + 2)
                    dve.wait_ge(la_phik, c + 1)
                    ve.tensor_scalar(min_t, ps[:, 4, :], bq_c, 0.0, ALU.add, ALU.min).then_inc(la_qmin, 1)
                    dve.wait_ge(la_kv, c + 2)
                    kv = ps[:, 5:7, :].rearrange("p a (i n) -> p (a i) n", n=2 * P)
                    ve.tensor_tensor(kz.rearrange("p (i n) -> p i n", i=4), kv[:, :, 0:P],
                                     bkv[:, 0:1, :].broadcast_to([P, 4, P]), ALU.add).then_inc(la_kb, 1)
                    ve.tensor_tensor(Vo[:, :, 0:P], kv[:, :, P:],
                                     bkv[:, 1:2, :].broadcast_to([P, 4, P]), ALU.add)
                    dve.wait_ge(la_kb, c + 2)
                    dve.wait_ge(la_phiq, c + 2)
                    ve.tensor_scalar(min_t, kz, 0.0, None, ALU.min).then_inc(la_kmin, 1)
                dve.wait_ge(la_sum, b + 2)
                ve.tensor_tensor(KVbd, ps[:, 7, 0:P], blocks, ALU.mult)
                ve.tensor_scalar(Zbd, blocks, ps[:, 7, P:P + 1], None, ALU.mult).then_inc(la_bd, 1)
                for cc in range(CPB):
                    c = b * CPB + cc
                    dve.wait_ge(la_den, c + 2)
                    ve.tensor_scalar(rden, ps[:, 4, :], LA_EPS, None, ALU.add).then_inc(la_rden, 1)
                    dve.wait_ge(la_rden, 2 * c + 2)
                    ve.reciprocal(rden, rden).then_inc(la_rden, 1)
                    dve.wait_ge(la_rden, 2 * c + 3)
                    ve.tensor_tensor(att, ps[:, 3, :], rden, ALU.mult).then_inc(la_att, 1)
                    n = b * 6 + 2 + 2 * cc
                    ln_a(n)
                    ln_b(n, xn[:, 1, :])
                    dve.wait_ge(ln_out, n + 2)
                    ve.tensor_tensor(x1[:, bass.ds(c * CH, CH)], x1[:, bass.ds(c * CH, CH)], xn[:, 1, :],
                                     ALU.add).then_inc(la_x1, 1)
                    ln_a(n + 1)
                    ln_b(n + 1, xin[:, bass.ds(ccol(c), CH)])

            def shift(dst, src, col, width):
                ve.tensor_copy(dst[0:64, :], src[0:64, bass.ds(col, width)])
                return ve.tensor_copy(dst[64:P, :], src[64:P, bass.ds(col - 1, width)])

            def products(l, t, p, h):
                dve.wait_ge(sq_done[h], l * TILES + t + 2)
                if not (isinstance(t, int) and t == 0):
                    dve.wait_ge(tk_done[h], l * TILES + t)
                dve.wait_ge(add_done[h], l * TILES + t + 1)
                tab = rot_tab[:, bass.ds(t % TPB, 1), :, :].rearrange("p a s n -> p (a s) n")
                qk = ps[:, 0:2, :].rearrange("p a (h d) -> p a h d", d=HD)
                ve.tensor_tensor(rotA[:, p, h, :].rearrange("p (a h d) -> p a h d", a=2, d=HD), qk,
                                 tab[:, 0, :].rearrange("p (a d) -> p a d", a=2).unsqueeze(2).broadcast_to([P, 2, 8, HD]),
                                 ALU.mult)
                swapped = ps[:, 0:2, :].rearrange("p a (h x f) -> p (a h) x f", x=2, f=32)[:, :, ::-1, :]
                ve.tensor_tensor(rotB[:, h, :].rearrange("p (a h d) -> p a h d", a=2, d=HD), swapped,
                                 tab[:, 1, :].rearrange("p (a d) -> p a d", a=2).unsqueeze(2).broadcast_to([P, 2, 8, HD]),
                                 ALU.mult).then_inc(prod_done[h], 1)

            def square_sums(h):
                ve.tensor_reduce(nrm[:, h, :], sq[:, h, :].rearrange("p (a d) -> p a d", d=HD), AX.X,
                                 ALU.add).then_inc(nrm_done[h], 1)

            def guess(l, t):
                dve.wait_ge(nrm_done[1], l * TILES + t + 2)
                dve.wait_ge(r_done, l * TILES + t + 1)
                ve.tensor_scalar(nsq[:], nrm[:], L2_EPS * L2_EPS, None, ALU.max).then_inc(nsq_done, 1)
                dve.wait_ge(nsq_done, l * TILES + t + 2)
                ve.tensor_scalar(nhalf[:], nsq[:], -0.5, None, ALU.mult)
                ve.tensor_scalar(rinv[:].bitcast(I32), nsq[:].bitcast(I32), -0.5, RSQRT_BITS,
                                 ALU.mult, ALU.add).then_inc(guess_done, 1)

            def sums(l, t, p):
                dve.wait_ge(exp_done, l * TILES + t + 2)
                ve.tensor_reduce(ssum[:], prob[:, p], AX.X, ALU.add).then_inc(sum_done, 1)
                dve.wait_ge(sum_done, l * TILES + t + 2)
                ve.reciprocal(rsum[:], ssum[:]).then_inc(rs_done, 1)

            def build_xs(l, t, p):
                if not (isinstance(t, int) and t == 0):
                    dve.wait_ge(qk_done[1], l * TILES + t)
                    dve.wait_ge(xsv_done, l * TILES + t)
                shift(xs[:, p, :], xin, tcol(t), P).then_inc(xs_done, 1)

            def spread(l, t, p):
                dve.wait_ge(norm_done, l * TILES + t + 2)
                if not (isinstance(t, int) and t == 0):
                    dve.wait_ge(av_done[1], l * TILES + t)
                for w in range(NW):
                    q0 = WIN * w
                    ve.transpose(PT[q0:q0 + WIN, p, :, q0:q0 + WIN], prob[q0:q0 + WIN, p, :, WIN:])
                    if w:
                        last = ve.transpose(PT[q0 - WIN:q0, p, :, q0:q0 + WIN], prob[q0:q0 + WIN, p, :, 0:WIN])
                    else:
                        ve.transpose(PTp[P - WIN:P, p, :, 0:WIN], prob[0:WIN, p, :, 0:WIN])
                last.then_inc(pt_done, 1)

            def maxima(l, t, p):
                dve.wait_ge(s_done, l * TILES + t + 2)
                ve.tensor_reduce(mx[:], ps[:, 4:6, :].rearrange("p e (a n) -> p (e a) n", n=2 * WIN), AX.X,
                                 ALU.max).then_inc(mx_done, 1)
                dve.wait_ge(mx_done, l * TILES + t + 2)
                dve.wait_ge(r_done, l * TILES + t + 2)
                ve.scalar_tensor_tensor(mxn[:].rearrange("p (e h a) -> p e h a", e=2, h=2),
                                        mx[:].rearrange("p (e h a) -> p e h a", e=2, h=2), -1.0,
                                        rq[:, p, :, :].rearrange("p h (a e) -> p e h a", e=2),
                                        ALU.mult, ALU.mult).then_inc(mxn_done, 1)

            def residual(l, t):
                dve.wait_ge(y_done, l * TILES + t + 2)
                col = tcol(t)
                ve.tensor_tensor(xmid[:, bass.ds(col, P)], ps[:, Y_BANK, 0:P], xin[:, bass.ds(col, P)],
                                 ALU.add).then_inc(xmid_done, 1)

            def slot(l, s, p, qk, score, av, y, more):
                if qk:
                    products(l, s, p, 0)
                if y:
                    residual(l, s - 4)
                if more:
                    build_xs(l, s + 1, 1 - p)
                if qk:
                    square_sums(0)
                if av:
                    sums(l, s - 2, p)
                if qk:
                    products(l, s, p, 1)
                    square_sums(1)
                    guess(l, s)
                if score:
                    maxima(l, s - 1, 1 - p)
                if av:
                    spread(l, s - 2, p)

            with dve.Fori(0, DEPTH) as l:
                dve.wait_ge(xout_done, l * CHUNKS + 1)
                dve.wait_ge(ln_out, LN_PRE + l * CHUNKS + 1)
                dve.wait_ge(tab_done, l + 2)
                build_xs(l, 0, 0)
                slot(l, 0, 0, True, False, False, False, True)
                slot(l, 1, 1, True, True, False, False, True)
                slot(l, 2, 0, True, True, True, False, True)
                slot(l, 3, 1, True, True, True, False, True)
                with dve.Fori(0, TILES // 2 - 3) as j:
                    for p in range(2):
                        slot(l, 2 * j + 4 + p, p, True, True, True, True, True)
                slot(l, TILES - 2, 0, True, True, True, True, True)
                slot(l, TILES - 1, 1, True, True, True, True, False)
                slot(l, TILES, 0, False, True, True, True, False)
                slot(l, TILES + 1, 1, False, False, True, True, False)
                slot(l, TILES + 2, 0, False, False, False, True, False)
                slot(l, TILES + 3, 1, False, False, False, True, False)
                dve.wait_ge(s_wffn, l * N_WFFN + N_WFFN)
                dve.wait_ge(xmid_done, l * TILES + TILES + 1)
                n = LN_PRE + l * CHUNKS
                shift(xsf, xmid, ccol(0), CH).then_inc(xsf_done, 1)
                ln_a(n)
                ln_b(n, xn[:, 0, :], True)
                for c in range(CHUNKS):
                    more = c + 1 < CHUNKS
                    if more:
                        dve.wait_ge(ln_cen, n + c + 2)
                        shift(xsf, xmid, ccol(c + 1), CH).then_inc(xsf_done, 1)
                    for m, (_, fb) in enumerate(FBLK):
                        k = 3 * c + m
                        dve.wait_ge(gl_done, l * 12 + k + 2)
                        if m == 0:
                            dve.wait_ge(f_done, l * CHUNKS + c + 1)
                        ve.scalar_tensor_tensor(hm[0:fb, m, :], ps[0:fb, 3 + k % 2, :], b1a[0:fb, m:m + 1],
                                                gl[0:fb, k % 2, :], ALU.add, ALU.mult).then_inc(hm_done, 1)
                        if more and m == 0:
                            ln_a(n + c + 1)
                        if more and m == 1:
                            ln_b(n + c + 1, xn[:, (c + 1) % 2, :], True)
                    dve.wait_ge(f_done, l * CHUNKS + c + 2)
                    col = ccol(c)
                    ve.scalar_tensor_tensor(xin[:, col:col + CH], ps[:, 7, :], b2c[:], xmid[:, col:col + CH],
                                            ALU.add, ALU.add).then_inc(xout_done, 1)

            with dve.Fori(0, CHUNKS) as c:
                ln_a(LN_FIN + c)
                dve.wait_ge(fin_T, c + 1)
                ln_b(LN_FIN + c, xn[:, 0, :])
                dve.wait_ge(ln_out, LN_FIN + c + 2)
                ve.tensor_tensor(xn[:, 0, :], xn[:, 0, :], x1[:, bass.ds(c * CH, CH)], ALU.add).then_inc(fin_add, 1)
                dve.wait_ge(fin_T, c + 2)
                dve.wait_ge(s_out, 16 * c + 16)
                ve.tensor_copy(ost, ps[:, 3, :].rearrange("p (i f) -> p i f", i=4)).then_inc(fin_copied, 1)

        @block.tensor
        def _(pe):
            te = nc.tensor

            def mm(o, lhsT, rhs, start=True, stop=True, **kw):
                return te.matmul(o, lhsT, rhs, start=start, stop=stop, **kw)

            def tr(o, i):
                return te.matmul(o, i, ident, start=True, stop=True, is_transpose=True)

            def ln_a(n, src):
                mm(ps[:, 0, :], centre, src).then_inc(ln_cen, 1)

            def ln_b(n):
                pe.wait_ge(ln_sq, n + 2)
                for i in range(4):
                    ins = mm(ps[:, 1, i:i + 1], ln_sqb[:, i * P:(i + 1) * P], ones_m[:, 0:1])
                ins.then_inc(ln_var, 1)

            def ln_c(n):
                pe.wait_ge(ln_pow, n + 2)
                pe.wait_ge(ln_out, n + 1)
                for i in range(4):
                    ins = tr(ps[:, 2, i * P:(i + 1) * P], ln_r[:, i:i + 1].broadcast_to([P, P]))
                ins.then_inc(ln_bc, 1)

            pe.wait_ge(s_const, 48)
            pe.wait_ge(s_wla, 64)
            for i in range(4):
                ins = tr(ps[:, 3, i * P:(i + 1) * P], wnat[:, i, :])
            ins.then_inc(wT_done, 1)
            pe.wait_ge(wT_copied, 1)
            with pe.Fori(0, B) as b:
                for cc in range(CPB):
                    c = b * CPB + cc
                    n = b * 6 + cc
                    pe.wait_ge(s_x, 16 * c + 16)
                    pe.wait_ge(la_att, b * CPB + 1)
                    for i in range(4):
                        ins = tr(ps[:, 3, i * P:(i + 1) * P], xst[:, i, :])
                    ins.then_inc(xT_done, 1)
                    pe.wait_ge(xT_copied, c + 2)
                    ln_a(n, x1[:, bass.ds(c * CH, CH)])
                    ln_b(n)
                    ln_c(n)
                    pe.wait_ge(ln_out, n + 2)
                    mm(ps[:, 4, :], wT[:, 0, :], xn[:, 0, :]).then_inc(la_q, 1)
                    for i in range(4):
                        ins = mm(ps[:, 5 + i // 2, (i % 2) * 256:(i % 2) * 256 + 256], xn[:, 0, i * P:(i + 1) * P],
                                 wT[:, 1:3, :].rearrange("p a n -> p (a n)"))
                    ins.then_inc(la_kv, 1)
                    pe.wait_ge(la_phik, c + 2)
                    for i in range(4):
                        ins = mm(ps[:, 7, 0:P + 1], phiK[:, i * P:(i + 1) * P], Vo[:, i, 0:P + 1],
                                 start=(cc == 0 and i == 0), stop=(cc == CPB - 1 and i == 3))
                    if cc == CPB - 1:
                        ins.then_inc(la_sum, 1)
                pe.wait_ge(la_bd, b + 2)
                for cc in range(CPB):
                    c = b * CPB + cc
                    n = b * 6 + 2 + 2 * cc
                    pe.wait_ge(la_att, c + 1)
                    mm(ps[:, 3, :], KVbd, phiQ[:, cc, :]).then_inc(la_num, 1)
                    mm(ps[:, 4, :], Zbd, phiQ[:, cc, :]).then_inc(la_den, 1)
                    pe.wait_ge(la_att, c + 2)
                    mm(ps[:, 5, :], wT[:, 3, :], att).then_inc(la_y, 1)
                    pe.wait_ge(la_ysb, c + 2)
                    ln_a(n, ysb)
                    ln_b(n)
                    ln_c(n)
                    pe.wait_ge(la_x1, c + 2)
                    ln_a(n + 1, x1[:, bass.ds(c * CH, CH)])
                    ln_b(n + 1)
                    ln_c(n + 1)

            def qk(l, t, p, h):
                if h == 0:
                    pe.wait_ge(xs_done, l * TILES + t + 2)
                pe.wait_ge(prod_done[1 - h], l * TILES + t + h + 1)
                pe.wait_ge(sq_done[1 - h], l * TILES + t + h + 1)
                for a in range(2):
                    o = a * INNER + h * HALF
                    ins = mm(ps[:, a, :], xs[:, p, :], wqkv[:, o:o + HALF])
                ins.then_inc(qk_done[h], 1)

            def tq(l, t, p, h):
                if h and not (isinstance(t, int) and t < 2):
                    pe.wait_ge(v_evac[1], l * TILES + t)
                pe.wait_ge(add_done[h], l * TILES + t + 2)
                for i in range(4):
                    ins = tr(ps[:, TQ_BANK[h], i * P:(i + 1) * P], rotA[:, p, h, i * P:(i + 1) * P])
                ins.then_inc(tq_done[h], 1)

            def tk(l, t, p, h):
                pe.wait_ge(tq_evac[1 - h], l * TILES + t + 2)
                pe.wait_ge(kmul_done, l * TILES + t + 2)
                for i in range(4):
                    ins = tr(ps[:, TK_BANK[h], i * P:(i + 1) * P], rotA[:, p, h, HALF + i * P:HALF + (i + 1) * P])
                ins.then_inc(tk_done[h], 1)

            def v(l, t, p, h):
                if h == 0:
                    pe.wait_ge(xsv_done, l * TILES + t + 2)
                    pe.wait_ge(o_evac[0], l * TILES + t + 1)
                o = 2 * INNER + h * HALF
                mm(ps[:, V_BANK[h], :], xsv[:, p, :], wqkv[:, o:o + HALF]).then_inc(v_done[h], 1)

            def scores(l, t):
                pe.wait_ge(exp_done, l * TILES + t + 1)
                for e in range(2):
                    if e:
                        pe.wait_ge(tk_evac[1], l * TILES + t + 2)
                    mm(ps[:, 4 + e, :], ident_b[:], mask[:, bass.ds(t, 1), :].broadcast_to([P, PAIRS, 2 * WIN]),
                       stop=False, skip_group_check=True)
                for a in range(PAIRS):
                    for w in range(NW):
                        for e in range(2):
                            ins = mm(ps[WIN * w:WIN * w + WIN, 4 + e, a * 64:a * 64 + 64],
                                     qT[64 * e:64 * e + 64, a, WIN * w:WIN * w + WIN],
                                     kT[64 * e:64 * e + 64, a, WIN * w:WIN * w + 2 * WIN],
                                     start=False, stop=True, skip_group_check=True)
                ins.then_inc(s_done, 1)

            def av(l, t, p, h):
                if h == 0:
                    pe.wait_ge(v_evac[1], l * TILES + t + 2)
                    pe.wait_ge(pt_done, l * TILES + t + 2)
                for i in range(4):
                    for e in range(2):
                        a = 4 * h + i
                        o = (2 * a + e) * HD
                        mm(ps[64 * e:64 * e + 64, O_BANK[h], i * P:(i + 1) * P], V[:, p, o:o + HD],
                           PT[:, p, e * PAIRS + a, :], start=(i == 0), skip_group_check=True)
                for i in range(4):
                    for e in range(2):
                        a = 4 * h + i
                        o = (2 * a + e) * HD
                        ins = mm(ps[64 * e:64 * e + 64, O_BANK[h], i * P:i * P + 2 * WIN], V[P - WIN:P, 1 - p, o:o + HD],
                                 PTp[P - WIN:P, p, e * PAIRS + a, :], start=False, skip_group_check=True)
                ins.then_inc(av_done[h], 1)

            def project(l, t):
                pe.wait_ge(o_evac[0], l * TILES + t + 2)
                pe.wait_ge(o_evac[1], l * TILES + t + 2)
                pe.wait_ge(xmid_done, l * TILES + t + 1)
                for a in range(PAIRS):
                    ins = mm(ps[:, Y_BANK, 0:P], wo[:, a, :], oT[:, a, :], start=(a == 0), stop=(a == PAIRS - 1))
                ins.then_inc(y_done, 1)

            def slot(l, s, p, score, av_v, o, has_qk=True, qk_next=True):
                if o:
                    av(l, s - 3, 1 - p, 0)
                if has_qk:
                    qk(l, s, p, 1)
                if score:
                    tk(l, s - 1, 1 - p, 0)
                    tk(l, s - 1, 1 - p, 1)
                    scores(l, s - 1)
                if o:
                    av(l, s - 3, 1 - p, 1)
                if av_v:
                    v(l, s - 2, p, 0)
                    v(l, s - 2, p, 1)
                if qk_next:
                    qk(l, s + 1, 1 - p, 0)
                if o:
                    project(l, s - 3)
                if has_qk:
                    tq(l, s, p, 0)
                    tq(l, s, p, 1)

            pe.wait_ge(init_v, 4)
            pe.wait_ge(init_p, 4)
            with pe.Fori(0, DEPTH) as l:
                pe.wait_ge(s_wattn, l * N_WATTN + N_WATTN)
                qk(l, 0, 0, 0)
                slot(l, 0, 0, False, False, False)
                slot(l, 1, 1, True, False, False)
                slot(l, 2, 0, True, True, False)
                with pe.Fori(0, TILES // 2 - 2) as j:
                    for i in range(2):
                        slot(l, 2 * j + 3 + i, 1 - i, True, True, True)
                slot(l, TILES - 1, 1, True, True, True, True, False)
                slot(l, TILES, 0, True, True, True, False, False)
                slot(l, TILES + 1, 1, False, True, True, False, False)
                slot(l, TILES + 2, 0, False, False, True, False, False)
                pe.wait_ge(s_wffn, l * N_WFFN + N_WFFN)
                n = LN_PRE + l * CHUNKS
                pe.wait_ge(xsf_done, l * CHUNKS + 2)
                ln_a(n, xsf[:])
                ln_b(n)
                ln_c(n)
                for c in range(CHUNKS):
                    more = c + 1 < CHUNKS
                    if more:
                        pe.wait_ge(xsf_done, l * CHUNKS + c + 3)
                        ln_a(n + c + 1, xsf[:])
                    pe.wait_ge(ln_out, n + c + 2)
                    for m, (o, fb) in enumerate(FBLK):
                        k = 3 * c + m
                        if k >= 2:
                            pe.wait_ge(hm_done, l * 12 + k)
                        mm(ps[0:fb, 3 + k % 2, :], w1[:, o:o + fb], xn[:, c % 2, :])
                        mm(ps[0:fb, 5 + k % 2, :], w1[:, FF + o:FF + o + fb], xn[:, c % 2, :]).then_inc(h_done, 1)
                        if more and m == 0:
                            ln_b(n + c + 1)
                        if more and m == 1:
                            ln_c(n + c + 1)
                    if c:
                        pe.wait_ge(xout_done, l * CHUNKS + c + 1)
                    pe.wait_ge(hm_done, l * 12 + 3 * c + 4)
                    for m, (o, fb) in enumerate(FBLK):
                        ins = mm(ps[:, 7, :], w2[0:fb, m, :], hm[0:fb, m, :], start=(m == 0), stop=(m == 2))
                    ins.then_inc(f_done, 1)

            pe.wait_ge(xout_done, DEPTH * CHUNKS + 1)
            with pe.Fori(0, CHUNKS) as c:
                ln_a(LN_FIN + c, xin[:, bass.ds(ccol(c), CH)])
                ln_b(LN_FIN + c)
                ln_c(LN_FIN + c)
                pe.wait_ge(fin_add, c + 2)
                pe.wait_ge(fin_copied, c + 1)
                for i in range(4):
                    ins = tr(ps[:, 3, i * P:(i + 1) * P], xn[:, 0, i * P:(i + 1) * P])
                ins.then_inc(fin_T, 1)


_INS = ['L0_attn_x', 'L0_attn_Wq', 'L0_attn_bq', 'L0_attn_Wk', 'L0_attn_bk', 'L0_attn_Wv', 'L0_attn_bv',
        'L0_attn_Wo', 'L0_attn_bo', 'L0_ffn_Wqkv', 'L0_ffn_q_scale', 'L0_ffn_k_scale', 'L0_ffn_Wo',
        'L0_ffn_ln_g', 'L0_ffn_ln_b', 'L0_ffn_W1', 'L0_ffn_b1', 'L0_ffn_W2', 'L0_ffn_b2']


def _constants():
    import numpy as np

    i = np.arange(P)
    mats = np.stack([np.eye(P), np.eye(P) - 1.0 / P, (i[:, None] // LA_HD == i[None, :] // LA_HD),
                     np.full((P, P), 1.0 / P)], 1).astype(np.float32)
    half = np.arange(0, HD, 2, dtype=np.float32)
    inv_freq = (np.float32(1.0) / np.float32(10000.0) ** (half / np.float32(HD))).astype(np.float32)
    pos = np.arange(N, dtype=np.float32)
    freqs = pos[:, None] * inv_freq[None, :]
    base = (half + np.float32(0.4 * HD)) / np.float32(1.4 * HD)
    power = (pos - N // 2) / np.float32(WIN // 2)
    scale = (base[None, :] ** power[:, None]).astype(np.float32)
    cos, sin = np.cos(freqs), np.sin(freqs)
    both = []
    for s in (scale, np.float32(1.0) / scale):
        both.append((np.concatenate([cos * s, cos * s], 1), np.concatenate([-sin * s, sin * s], 1)))
    rot = np.stack([np.concatenate([both[0][k], both[1][k]], 1) for k in range(2)], 1)
    rot = rot.reshape(TPB, P, 2, P).transpose(1, 0, 2, 3).astype(np.float32)
    q, j = np.arange(P)[:, None] % WIN, np.arange(2 * WIN)[None, :]
    seen = (j >= q) & (j <= q + WIN)
    first = seen & ~((np.arange(P)[:, None] < WIN) & (j < WIN))
    mask = np.where(np.stack([first, seen], 1), 0.0, -1e30).astype(np.float32)
    return {"c_mats": mats, "c_rot": rot, "c_mask": mask}


def kernel(**inputs):
    import numpy as np
    import concourse.bacc as bacc
    from concourse.bass_utils import run_bass_kernel_spmd

    nc = bacc.Bacc("TRN2", target_bir_lowering=False, num_devices=1)
    arrays, args = {}, []
    given = {name: np.ascontiguousarray(inputs[name]) for name in _INS}
    given.update({k: np.ascontiguousarray(a) for k, a in _constants().items()})
    for name, a in given.items():
        arrays[f"in_{name}"] = a
        args.append(nc.dram_tensor(f"in_{name}", a.shape, mybir.dt.from_np(a.dtype), kind="ExternalInput").ap())
    o = nc.dram_tensor("out_0", (B, N, P), F32, kind="ExternalOutput").ap()
    program(nc, *args, o)
    r = run_bass_kernel_spmd(nc, [arrays], core_ids=[0])
    return r.results[0]["out_0"]
```

```python
import concourse.bass as bass
from concourse import mybir
from concourse.alu_op_type import AluOpType as ALU
from contextlib import ExitStack

F32 = mybir.dt.float32
BF16 = mybir.dt.bfloat16
I32 = mybir.dt.int32
F32R = mybir.dt.float32r
ACT = mybir.ActivationFunctionType
AX = mybir.AxisListType

P = 128
B, N = 2, 1024
TOK = B * N
TILES = TOK // P
TPB = TILES // B
CH = 512
CHUNKS = TOK // CH
CPB = CHUNKS // B
DEPTH, HEADS, HD, WIN = 6, 16, 64, 32
INNER = HEADS * HD
PAIRS = HEADS // 2
HALF = INNER // 2
FF = 341
FB = 114
FBLK = [(0, 114), (114, 114), (228, 113)]
NW = P // WIN
LA_HD = 8
LA_EPS, LN_EPS, L2_EPS = 1e-6, 1e-5, 1e-12
RSQRT_BITS = 1597463007.0
TQ_BANK, TK_BANK, V_BANK, O_BANK, Y_BANK = (2, 3), (3, 6), (7, 3), (7, 2), 6


def tcol(t):
    return t * P + t // TPB + 1


def ccol(c):
    return c * CH + c // CPB + 1


def program(nc, x, Wq, bq, Wk, bk, Wv, bv, Wo, bo, Wqkv, q_scale, k_scale, Wo6, ln_g, ln_b,
            W1, b1, W2, b2, c_mats, c_rot, c_mask, out):
    ctx = ExitStack()
    with ctx:
        def sb(name, shape, dt=F32):
            return ctx.enter_context(nc.sbuf_tensor(name, shape, dt))

        def sem(name):
            return ctx.enter_context(nc.semaphore(name))

        seeded = []

        def cnt(name):
            seeded.append(sem(name))
            return seeded[-1]

        def cnt2(name):
            return [cnt(f"{name}{i}") for i in range(2)]

        mats = sb("mats", [P, 4, P])
        ident, centre, blocks, ones_m = (mats[:, i, :] for i in range(4))
        ident_b = sb("ident_b", [P, P], BF16)
        mask_f = sb("mask_f", [P, 2, HD])
        mask = sb("mask", [P, TILES, HD], BF16)
        keep = sb("keep", [P, TILES + 1])
        minus_half = sb("minus_half", [P, TILES])
        one_half = sb("one_half", [P, 2, HEADS])
        newt_z = sb("newt_z", [P, 2, HEADS])
        newt_u = sb("newt_u", [P, 2, HEADS])
        rot_base = sb("rot_base", [P, TPB, 2, P])
        rot_tab = sb("rot_tab", [P, TPB, 2, P])
        scales = sb("scales", [P, 2, P])
        x1 = sb("x1", [P, TOK])
        xin = sb("xin", [P, TOK + B + 2])
        xmid = sb("xmid", [P, TOK + B + 2])
        w_hi = sb("w_hi", [P, 3 * INNER], F32R)
        w_lo = sb("w_lo", [P, 3 * INNER], F32R)
        wo = sb("wo", [P, PAIRS, P])
        w1 = sb("w1", [P, 2 * FF])
        w2 = sb("w2", [FB, 3, P])
        lng = sb("lng", [P, 1])
        lnb = sb("lnb", [P, 1])
        b1a = sb("b1a", [FB, 3])
        b1g = sb("b1g", [FB, 3])
        b2c = sb("b2c", [P, 1])
        xs = sb("xs", [P, 2, P])
        x_hl = sb("x_hl", [P, 2, 2, P], F32R)
        xsv = sb("xsv", [P, 2, 2, P], F32R)
        sq = sb("sq", [P, 2, 2 * HALF])
        rotA = sb("rotA", [P, 2, 2, 2 * HALF])
        rotB = sb("rotB", [P, 2, 2 * HALF])
        nrm = sb("nrm", [P, 2, HEADS])
        nsq = sb("nsq", [P, 2, HEADS])
        nhalf = sb("nhalf", [P, 2, HEADS])
        rinv = sb("rinv", [P, 2, HEADS])
        rq = sb("rq", [P, 2, 2, 8])
        qT = sb("qT", [P, PAIRS, P])
        kT = sb("kT", [P, PAIRS, WIN + P])
        V = sb("V", [P, 2, INNER])
        prob = sb("prob", [P, 2, HEADS, 2 * WIN])
        mx = sb("mx", [P, HEADS])
        mxn = sb("mxn", [P, HEADS])
        ssum = sb("ssum", [P, HEADS])
        rsum = sb("rsum", [P, HEADS])
        PT = sb("PT", [P, 2, HEADS, P])
        PTp = sb("PTp", [P, 2, HEADS, 2 * WIN])
        oT = sb("oT", [P, PAIRS, P])
        ln_sqb = sb("ln_sqb", [P, CH])
        ln_xcb = sb("ln_xcb", [P, CH])
        ln_ve = sb("ln_ve", [P, 4])
        ln_r = sb("ln_r", [P, 4])
        l4_ve = sb("l4_ve", [P, TILES])
        l4_r = sb("l4_r", [P, TILES])
        xsf = sb("xsf", [P, CH])
        xn = sb("xn", [P, 2, CH])
        gl = sb("gl", [FB, 2, CH])
        hm = rotA[0:FB].rearrange("p t h n -> p t (h n)")[:, :, 0:3 * CH].rearrange("p t (m n) -> p t m n", m=3)
        ps = ctx.enter_context(nc.psum_tensor("ps", [P, 8, CH], F32))

        w_raw = [rotB[:, 0], rotB[:, 1], sq[:, 0]]

        wnat, wT = wo[:, 0:4, :], wo[:, 4:8, :]
        bq_c, bo_c = rsum[:, 0:1], rsum[:, 1:2]
        bkv = sb("bkv", [P, 2, P])
        x_rows = rot_tab[:].rearrange("p a b n -> p (a b n)").rearrange("p (c i f) -> p c i f", c=CHUNKS, i=4)
        centred = V[:].rearrange("p a (b n) -> p (a b) n", b=2)
        normed = rotA[:, 0].rearrange("p a (b n) -> p (a b) n", b=2)
        phiQ = rotA[:, 1].rearrange("p a (b n) -> p (a b) n", b=2)
        ysb = normed
        squares = [ln_sqb[:], xsf[:]]
        relu_q, min_q = xn, sq[:, 1].rearrange("p (b n) -> p b n", b=2)
        relu_k, min_k = (prob[:, i].rearrange("p a n -> p (a n)").rearrange("p (b n) -> p b n", b=2) for i in range(2))
        kz = qT[:].rearrange("p a n -> p (a n)").rearrange("p (b n) -> p b n", b=2)
        phiK = oT[:].rearrange("p a n -> p (a n)").rearrange("p (b n) -> p b n", b=2)
        Vo = rot_tab[:].rearrange("p a b n -> p (a b n)")[:, 0:8 * 130].rearrange("p (b i n) -> p b i n", b=2, i=4)
        rden = xmid[:, 1:1 + 2 * CH].rearrange("p (b n) -> p b n", b=2)
        bd = xmid[:, 2 + 2 * CH:2 + 2 * CH + 4 * P].rearrange("p (b s n) -> p b s n", b=2, s=2)
        att = xn

        s_const, s_bias, s_wla, s_x, s_out = map(sem, ["s_const", "s_bias", "s_wla", "s_x", "s_out"])
        s_wattn, s_wffn = sem("s_wattn"), sem("s_wffn")
        init_v, init_p = sem("init_v"), sem("init_p")
        wT_done, wT_copied, xT_done, xT_copied = map(sem, ["wT_done", "wT_copied", "xT_done", "xT_copied"])
        l4_cen, l4_sq, l4_var, l4_eps, l4_pow, l4_bc, l4_out = map(
            sem, ["l4_cen", "l4_sq", "l4_var", "l4_eps", "l4_pow", "l4_bc", "l4_out"])
        la_q, la_qmin, la_qexp, la_phiq, la_kv, la_kb, la_v, la_kmin, la_kexp, la_phik = map(
            sem, ["la_q", "la_qmin", "la_qexp", "la_phiq", "la_kv", "la_kb", "la_v", "la_kmin", "la_kexp", "la_phik"])
        la_sum, la_bd, la_den, la_eps, la_rden, la_att, la_y, la_ysb, la_x1 = map(
            sem, ["la_sum", "la_bd", "la_den", "la_eps", "la_rden", "la_att", "la_y", "la_ysb", "la_x1"])
        fin_add, fin_T, fin_copied = map(sem, ["fin_add", "fin_T", "fin_copied"])
        ln_cen, ln_sq, ln_var, ln_eps, ln_pow, ln_bc, ln_mul, ln_out = map(
            cnt, ["ln_cen", "ln_sq", "ln_var", "ln_eps", "ln_pow", "ln_bc", "ln_mul", "ln_out"])
        tab_done = cnt("tab_done")
        xs_done, xhi_done, xlo_done, xsv_done, whi_done, wlo_done = map(
            cnt, ["xs_done", "xhi_done", "xlo_done", "xsv_done", "whi_done", "wlo_done"])
        qk_done, sq_done, prod_done = map(cnt2, ["qk_done", "sq_done", "prod_done"])
        nsq_done = cnt("nsq_done")
        add_done = cnt2("add_done")
        kmul_done, r_done, guess_done, newton, newton_y = map(cnt, ["kmul_done", "r_done", "guess_done", "newton", "newton_y"])
        nrm_done = cnt2("nrm_done")
        tq_done, tq_evac, tk_done, tk_evac = map(cnt2, ["tq_done", "tq_evac", "tk_done", "tk_evac"])
        kprev = cnt("kprev")
        v_done, v_evac, av_done, o_evac = map(cnt2, ["v_done", "v_evac", "av_done", "o_evac"])
        s_done, mx_done, mxn_done, exp_done, sum_done, rs_done, norm_done, pt_done, y_done, xmid_done = map(
            cnt, ["s_done", "mx_done", "mxn_done", "exp_done", "sum_done", "rs_done", "norm_done",
                  "pt_done", "y_done", "xmid_done"])
        xsf_done, h_done, gl_done, hm_done, f_done, xout_done = map(
            cnt, ["xsf_done", "h_done", "gl_done", "hm_done", "f_done", "xout_done"])

        block = ctx.enter_context(nc.Block())

        @block.sync
        def _(sp):
            for counter in seeded:
                sp.sem_inc(counter, 1)
            xr = x.rearrange("b (c i p) f -> (b c) p i f", i=4, p=P)
            sp.dma_start(mats[:], c_mats).then_inc(s_const, 16)
            for c in range(CHUNKS):
                sp.dma_start(x_rows[:, c], xr[c]).then_inc(s_x, 16)
            sp.dma_start(wnat[:, 0, :], Wq).then_inc(s_wla, 16)
            sp.dma_start(wnat[:, 1, :], Wk).then_inc(s_wla, 16)
            sp.dma_start(wnat[:, 2, :], Wv).then_inc(s_wla, 16)
            sp.dma_start(wnat[:, 3, :], Wo).then_inc(s_wla, 16)
            sp.dma_start(mask_f[:], c_mask).then_inc(s_const, 16)
            sp.dma_start(rot_base[:], c_rot).then_inc(s_const, 16)
            sp.dma_start(bq_c, bq.rearrange("(p a) -> p a", a=1)).then_inc(s_bias, 16)
            sp.dma_start(bo_c, bo.rearrange("(p a) -> p a", a=1)).then_inc(s_bias, 16)
            sp.dma_start(bkv[:, 0, :], bk.partition_broadcast(P)).then_inc(s_bias, 16)
            sp.dma_start(bkv[:, 1, :], bv.partition_broadcast(P)).then_inc(s_bias, 16)
            with sp.Fori(0, DEPTH) as l:
                sp.wait_ge(v_done[1], l * TILES + 1)
                for i in range(3):
                    sp.dma_start(w_raw[i], Wqkv[bass.ds(l, 1), :, i * INNER:(i + 1) * INNER]
                                 .rearrange("a p n -> (a p) n")).then_inc(s_wattn, 16)
                sp.wait_ge(tab_done, l + 1)
                for qk, s in ((0, q_scale), (1, k_scale)):
                    row = s[bass.ds(l, 1), :].rearrange("a d -> (a d)")
                    o = qk * HD
                    sp.dma_start(scales[:, 0, o:o + HD], row.partition_broadcast(P)).then_inc(s_wattn, 16)
                    sp.dma_start(scales[:, 1, o:o + 32], row[32:64].partition_broadcast(P)).then_inc(s_wattn, 16)
                    sp.dma_start(scales[:, 1, o + 32:o + 64], row[0:32].partition_broadcast(P)).then_inc(s_wattn, 16)
                sp.wait_ge(la_ysb, CHUNKS)
                sp.wait_ge(y_done, l * TILES + 1)
                sp.dma_start(wo[:], Wo6[bass.ds(l, 1), :, :].rearrange("a (k p) n -> (a p) k n", p=P)).then_inc(s_wattn, 16)
                sp.wait_ge(xout_done, l * CHUNKS + 1)
                sp.dma_start(w1[:], W1[bass.ds(l, 1), :, :].rearrange("a p n -> (a p) n")).then_inc(s_wffn, 16)
                w2l = W2[bass.ds(l, 1), :, :].rearrange("a k n -> (a k) n")
                b1l = b1[bass.ds(l, 1), :].rearrange("a n -> (a n)")
                sp.dma_start(w2[:, 0:2, :], w2l[0:228, :].rearrange("(m k) n -> k m n", m=2)).then_inc(s_wffn, 16)
                sp.dma_start(w2[0:113, 2, :], w2l[228:341, :]).then_inc(s_wffn, 16)
                for dst, o in ((b1a, 0), (b1g, FF)):
                    sp.dma_start(dst[:, 0:2], b1l[o:o + 228].rearrange("(m k) -> k m", m=2),
                                 allow_slow_non_contiguous=True).then_inc(s_wffn, 16)
                    sp.dma_start(dst[0:113, 2:3], b1l[o + 228:o + 341].rearrange("(k a) -> k a", a=1)).then_inc(s_wffn, 16)
                for dst, src in ((lng, ln_g), (lnb, ln_b), (b2c, b2)):
                    sp.dma_start(dst[:], src[bass.ds(l, 1), :].rearrange("a (p q) -> (a p) q", q=1)).then_inc(s_wffn, 16)
            outr = out.rearrange("b (c i p) f -> (b c) p i f", i=4, p=P)
            for c in range(CHUNKS):
                sp.wait_ge(fin_copied, c + 1)
                sp.dma_start(outr[c], x_rows[:, c]).then_inc(s_out, 16)
            sp.wait_ge(s_out, 16 * CHUNKS)
        N_WATTN, N_WFFN = 10 * 16, 10 * 16

        @block.gpsimd
        def _(pool):
            gp = nc.gpsimd
            gp.memset(minus_half[:], -0.5).then_inc(init_p, 1)
            gp.memset(one_half[:], 1.5)
            gp.memset(PTp[:], 0.0)
            gp.memset(PT[:], 0.0).then_inc(init_p, 1)
            gp.memset(kT[:], 0.0).then_inc(init_p, 1)
            pool.wait_ge(init_p, 3)

            def ln(n):
                pool.wait_ge(ln_eps, n + 2)
                gp.tensor_tensor(ln_r[:], ln_ve[:], minus_half[:, 0:4], ALU.pow).then_inc(ln_pow, 1)

            def ln4(k):
                pool.wait_ge(l4_eps, k + 1)
                gp.tensor_tensor(l4_r[:], l4_ve[:], minus_half[:], ALU.pow).then_inc(l4_pow, 1)

            ln4(0)
            for c in range(CHUNKS):
                pool.wait_ge(la_qexp, c + 1)
                gp.tensor_tensor(phiQ[:, c], relu_q[:, c % 2], min_q[:, c % 2], ALU.add).then_inc(la_phiq, 1)
                pool.wait_ge(la_kexp, c + 1)
                if c >= 2:
                    pool.wait_ge(la_sum, c - 1)
                gp.tensor_tensor(phiK[:, c % 2], relu_k[:, c % 2], min_k[:, c % 2], ALU.add).then_inc(la_phik, 1)
            def add(l, t, p, h):
                pool.wait_ge(prod_done[h], l * TILES + t + 2)
                gp.tensor_tensor(rotA[:, p, h, :], rotA[:, p, h, :], rotB[:, h, :], ALU.add).then_inc(add_done[h], 1)

            def newton_step(l, t, it):
                done = (l * TILES + t) * 9 + 3 * it + 1
                pool.wait_ge(newton_y, (l * TILES + t) * 3 + it + 1)
                gp.tensor_tensor(newt_z[:], rinv[:], rinv[:], ALU.mult).then_inc(newton, 1)
                pool.wait_ge(newton, done + 1)
                gp.tensor_tensor(newt_u[:], newt_z[:], nhalf[:], ALU.mult).then_inc(newton, 1)
                pool.wait_ge(newton, done + 2)
                gp.tensor_tensor(newt_z[:], newt_u[:], one_half[:], ALU.add).then_inc(newton, 1)
                pool.wait_ge(newton, done + 3)
                gp.tensor_tensor(rinv[:], newt_z[:], rinv[:], ALU.mult).then_inc(newton_y, 1)

            def scale_k(l, t, p):
                pool.wait_ge(newton_y, (l * TILES + t) * 3 + 4)
                kk = rotA[:, p, :, HALF:].rearrange("p h (a d) -> p h a d", d=HD)
                gp.tensor_tensor(kk, kk, rinv[:, :, 8:16].unsqueeze(3).broadcast_to([P, 2, 8, HD]),
                                 ALU.mult).then_inc(kmul_done, 1)
                gp.tensor_scalar(rq[:, p, :, :], rinv[:, :, 0:8], 8.0, None, ALU.mult).then_inc(r_done, 1)

            def normalise(l, t, p):
                pool.wait_ge(rs_done, l * TILES + t + 2)
                gp.tensor_tensor(prob[:, p], prob[:, p], rsum[:].unsqueeze(2).broadcast_to([P, HEADS, 2 * WIN]),
                                 ALU.mult).then_inc(norm_done, 1)

            def weights_low(l, i):
                pool.wait_ge(whi_done, 3 * l + i + 2)
                part = slice(i * INNER, (i + 1) * INNER)
                gp.tensor_tensor(w_lo[:, part], w_raw[i], w_hi[:, part].bitcast(F32), ALU.subtract).then_inc(wlo_done, 1)

            def x_low(l, t, p):
                pool.wait_ge(xhi_done, l * TILES + t + 2)
                gp.tensor_tensor(x_hl[:, p, 1, :], xs[:, p, :], x_hl[:, p, 0, :].bitcast(F32), ALU.subtract).then_inc(xlo_done, 1)

            def slot(l, s, p, qk, av, more=True):
                if qk:
                    add(l, s, p, 0)
                if av:
                    normalise(l, s - 2, p)
                if more:
                    x_low(l, s + 1, 1 - p)
                if qk:
                    add(l, s, p, 1)
                    pool.wait_ge(guess_done, l * TILES + s + 2)
                    newton_step(l, s, 0)
                    newton_step(l, s, 1)
                    newton_step(l, s, 2)
                    scale_k(l, s, p)

            def tables(l):
                pool.wait_ge(s_wattn, l * N_WATTN + N_WATTN)
                pool.wait_ge(prod_done[1], l * TILES + 1)
                for part in range(2):
                    ins = gp.tensor_tensor(rot_tab[:, :, part, :], rot_base[:, :, part, :],
                                           scales[:, part, :].unsqueeze(1).broadcast_to([P, TPB, P]), ALU.mult)
                ins.then_inc(tab_done, 1)

            def layer(l, more):
                slot(l, 1, 1, True, False)
                with pool.Fori(0, TILES // 2 - 2) as j:
                    for p in range(2):
                        slot(l, 2 * j + 2 + p, p, True, True)
                slot(l, TILES - 2, 0, True, True)
                slot(l, TILES - 1, 1, True, True, False)
                slot(l, TILES, 0, False, True, False)
                slot(l, TILES + 1, 1, False, True, False)
                for c in range(CHUNKS):
                    ln(l * CHUNKS + c)
                    if more and c == CHUNKS - 2:
                        weights_low(l + 1, 0)
                        weights_low(l + 1, 1)
                if more:
                    weights_low(l + 1, 2)
                    x_low(l + 1, 0, 0)
                    tables(l + 1)
                    slot(l + 1, 0, 0, True, False)

            ln4(1)
            for i in range(3):
                weights_low(0, i)
            pool.wait_ge(s_const, 48)
            tables(0)
            ln4(2)
            x_low(0, 0, 0)
            slot(0, 0, 0, True, False)
            with pool.Fori(0, DEPTH - 1) as l:
                layer(l, True)
            layer(DEPTH - 1, False)
            ln4(3)

        @block.scalar
        def _(act):
            ac = nc.scalar

            def ln(n):
                act.wait_ge(ln_cen, n + 2)
                act.wait_ge(ln_out, n + 1)
                ac.activation(ln_xcb[:], ps[:, 0, :], ACT.Copy)
                ac.activation(ln_sqb[:], ps[:, 0, :], ACT.Square).then_inc(ln_sq, 1)

            act.wait_ge(s_bias, 64)

            def ln4(k):
                for c in range(CHUNKS):
                    act.wait_ge(l4_cen, 4 * k + c + 1)
                    if k:
                        act.wait_ge(l4_out, 4 * k)
                    if c >= 2:
                        act.wait_ge(l4_var, 4 * k + c - 1)
                    ac.activation(centred[:, c], ps[:, c % 2, :], ACT.Copy)
                    ac.activation(squares[c % 2], ps[:, c % 2, :], ACT.Square).then_inc(l4_sq, 1)

            ln4(0)
            for c in range(CHUNKS):
                act.wait_ge(la_q, c + 1)
                act.wait_ge(la_qmin, c + 1)
                if c >= 2:
                    act.wait_ge(la_phiq, c - 1)
                ac.activation(relu_q[:, c % 2], ps[:, c % 2, :], ACT.Relu, bias=bq_c)
                ac.activation(min_q[:, c % 2], min_q[:, c % 2], ACT.Exp).then_inc(la_qexp, 1)
                act.wait_ge(la_kb, c + 1)
                if c >= 2:
                    act.wait_ge(la_phik, c - 1)
                ac.activation(relu_k[:, c % 2], kz[:, c % 2], ACT.Relu)
                act.wait_ge(la_kmin, c + 1)
                ac.activation(min_k[:, c % 2], min_k[:, c % 2], ACT.Exp).then_inc(la_kexp, 1)
            for c in range(CHUNKS):
                act.wait_ge(la_y, c + 1)
                ac.activation(ysb[:, c], ps[:, 4 + c % 2, :], ACT.Identity, bias=bo_c).then_inc(la_ysb, 1)
            def sq_unit(l, t, h):
                act.wait_ge(qk_done[h], l * TILES + t + 2)
                act.wait_ge(nrm_done[h], l * TILES + t + 1)
                ac.activation(sq[:, h, :], ps[:, 0:2, :].rearrange("p a n -> p (a n)"), ACT.Square).then_inc(sq_done[h], 1)

            def evac_tq(l, t, h):
                act.wait_ge(tq_done[h], l * TILES + t + 2)
                act.wait_ge(s_done, l * TILES + t + 1)
                ac.activation(qT[:, 4 * h:4 * h + 4, :], ps[:, TQ_BANK[h], :].rearrange("p (a n) -> p a n", a=4),
                              ACT.Copy).then_inc(tq_evac[h], 1)

            def evac_tk(l, t, h):
                act.wait_ge(kprev, l * TILES + t + 1)
                act.wait_ge(tk_done[h], l * TILES + t + 2)
                ac.activation(kT[:, 4 * h:4 * h + 4, WIN:], ps[:, TK_BANK[h], :].rearrange("p (a n) -> p a n", a=4),
                              ACT.Copy).then_inc(tk_evac[h], 1)

            def evac_v(l, t, p, h):
                act.wait_ge(v_done[h], l * TILES + t + 2)
                act.wait_ge(av_done[1], l * TILES + t + 1)
                ac.activation(V[:, p, h * HALF:(h + 1) * HALF], ps[:, V_BANK[h], :], ACT.Copy).then_inc(v_evac[h], 1)

            def evac_o(l, t, h):
                act.wait_ge(av_done[h], l * TILES + t + 2)
                act.wait_ge(y_done, l * TILES + t + 1)
                ac.activation(oT[:, 4 * h:4 * h + 4, :], ps[:, O_BANK[h], :].rearrange("p (a n) -> p a n", a=4),
                              ACT.Copy).then_inc(o_evac[h], 1)

            def exps(l, t, p, e):
                if e == 0:
                    act.wait_ge(mxn_done, l * TILES + t + 2)
                for a in range(PAIRS):
                    hh, ae = a // 4, 2 * (a % 4) + e
                    i = e * PAIRS + a
                    ins = ac.activation(prob[:, p, i, :], ps[:, 4 + e, a * 64:a * 64 + 64], ACT.Exp,
                                        bias=mxn[:, i:i + 1], scale=rq[:, p, hh, ae:ae + 1])
                if e:
                    ins.then_inc(exp_done, 1)

            def keep_window(l, t):
                ac.activation(kT[:, :, 0:WIN], kT[:, :, P:P + WIN], ACT.Copy,
                              scale=keep[:, bass.ds(t + 1, 1)]).then_inc(kprev, 1)

            def weights_high(l, i):
                act.wait_ge(s_wattn, l * N_WATTN + N_WATTN)
                part = slice(i * INNER, (i + 1) * INNER)
                ac.activation(w_hi[:, part], w_raw[i], ACT.Copy).then_inc(whi_done, 1)

            def x_high(l, t, p):
                act.wait_ge(xs_done, l * TILES + t + 2)
                if not (isinstance(t, int) and t == 0):
                    act.wait_ge(qk_done[1], l * TILES + t)
                    act.wait_ge(xsv_done, l * TILES + t)
                ac.activation(x_hl[:, p, 0, :], xs[:, p, :], ACT.Copy).then_inc(xhi_done, 1)

            def copy_xs(l, t, p):
                act.wait_ge(xlo_done, l * TILES + t + 2)
                if not (isinstance(t, int) and t < 2):
                    act.wait_ge(v_done[1], l * TILES + t)
                ac.activation(xsv[:, p], x_hl[:, p].bitcast(F32), ACT.Copy).then_inc(xsv_done, 1)

            def slot(l, s, p, score, av, o, qk=True, qk_next=True, norm=None):
                if norm is not None:
                    ln(l * CHUNKS + norm)
                if qk:
                    sq_unit(l, s, 1)
                if score:
                    evac_tk(l, s - 1, 0)
                    evac_tk(l, s - 1, 1)
                    copy_xs(l, s - 1, 1 - p)
                if o:
                    evac_o(l, s - 3, 0)
                if qk_next:
                    x_high(l, s + 1, 1 - p)
                if o:
                    evac_o(l, s - 3, 1)
                if score:
                    exps(l, s - 1, 1 - p, 0)
                if qk_next:
                    sq_unit(l, s + 1, 0)
                if av:
                    evac_v(l, s - 2, p, 0)
                    evac_v(l, s - 2, p, 1)
                if score:
                    exps(l, s - 1, 1 - p, 1)
                    keep_window(l, s - 1)
                if qk:
                    evac_tq(l, s, 0)
                    evac_tq(l, s, 1)

            ln4(1)
            for i in range(3):
                weights_high(0, i)
            ln4(2)
            act.wait_ge(init_p, 3)
            act.wait_ge(init_v, 5)
            def layer(l, more):
                slot(l, 1, 1, True, False, False)
                slot(l, 2, 0, True, True, False)
                with act.Fori(0, TILES // 2 - 2) as j:
                    for i in range(2):
                        slot(l, 2 * j + 3 + i, 1 - i, True, True, True)
                slot(l, TILES - 1, 1, True, True, True, True, False)
                slot(l, TILES, 0, True, True, True, False, False)
                slot(l, TILES + 1, 1, False, True, True, False, False, 0)
                slot(l, TILES + 2, 0, False, False, True, False, False, 1)
                act.wait_ge(s_wffn, l * N_WFFN + N_WFFN)
                for c in range(CHUNKS):
                    if 0 < c < CHUNKS - 1:
                        ln(l * CHUNKS + c + 1)
                    if more and c == CHUNKS - 1:
                        x_high(l + 1, 0, 0)
                    for m, (_, fb) in enumerate(FBLK):
                        k = 3 * c + m
                        act.wait_ge(h_done, l * 12 + k + 2)
                        if k >= 2:
                            act.wait_ge(hm_done, l * 12 + k)
                        ac.activation(gl[0:fb, k % 2, :], ps[0:fb, 5 + k % 2, :], ACT.Gelu,
                                      bias=b1g[0:fb, m:m + 1]).then_inc(gl_done, 1)
                        if more and c == 1:
                            weights_high(l + 1, m)
                        if more and c == CHUNKS - 1 and m == 0:
                            sq_unit(l + 1, 0, 0)
                if more:
                    slot(l + 1, 0, 0, False, False, False)

            x_high(0, 0, 0)
            sq_unit(0, 0, 0)
            slot(0, 0, 0, False, False, False)
            with act.Fori(0, DEPTH - 1) as l:
                layer(l, True)
            layer(DEPTH - 1, False)
            ln4(3)
            for c in range(CHUNKS):
                act.wait_ge(fin_T, c + 1)
                ac.activation(x_rows[:, c], ps[:, c, :].rearrange("p (i f) -> p i f", i=4), ACT.Copy).then_inc(fin_copied, 1)

        @block.vector
        def _(dve):
            ve = nc.vector
            dve.wait_ge(s_const, 48)
            ve.tensor_copy(ident_b[:], ident)
            ve.tensor_copy(mask[:], mask_f[:, 1:2, :].broadcast_to([P, TILES, HD])).then_inc(init_v, 1)
            dve.wait_ge(init_v, 1)
            ve.tensor_copy(mask[:, 0:TILES:TPB, :], mask_f[:, 0:1, :].broadcast_to([P, B, HD])).then_inc(init_v, 1)
            ve.memset(keep[:], 1.0)
            ve.memset(xin[:], 0.0).then_inc(init_v, 1)
            ve.memset(xmid[:], 0.0).then_inc(init_v, 1)
            dve.wait_ge(init_v, 4)
            ve.memset(keep[:, 0:TILES + 1:TPB], 0.0).then_inc(init_v, 1)

            def ln_a(n):
                dve.wait_ge(ln_var, n + 2)
                ve.tensor_scalar(ln_ve[:], ps[:, 1, 0:4], LN_EPS, None, ALU.add).then_inc(ln_eps, 1)

            def ln_b(n, dst):
                dve.wait_ge(ln_bc, n + 2)
                ve.tensor_tensor(dst, ps[:, 1, :], ln_xcb[:], ALU.mult).then_inc(ln_mul, 1)
                dve.wait_ge(ln_mul, n + 2)
                ve.tensor_scalar(dst, dst, lng[:], lnb[:], ALU.mult, ALU.add).then_inc(ln_out, 1)

            def eps4(k):
                dve.wait_ge(l4_var, 4 * k + 4)
                ve.tensor_scalar(l4_ve[:], ps[:, 2, 0:TILES], LN_EPS, None, ALU.add).then_inc(l4_eps, 1)

            def norm4(k, c, dst):
                dve.wait_ge(l4_bc, 4 * k + c + 1)
                ve.tensor_tensor(dst, ps[:, 4 + c, :], centred[:, c], ALU.mult).then_inc(l4_out, 1)

            for c in range(CHUNKS):
                dve.wait_ge(xT_done, c + 1)
                ve.tensor_copy(x1[:, c * CH:(c + 1) * CH], ps[:, 4 + c, :]).then_inc(xT_copied, 1)
            dve.wait_ge(wT_done, 1)
            ve.tensor_copy(wT, ps[:, 3, :].rearrange("p (a n) -> p a n", a=4)).then_inc(wT_copied, 1)
            dve.wait_ge(s_bias, 64)
            dve.wait_ge(xT_done, CHUNKS)
            ve.memset(Vo[:, :, :, P:P + 2], 1.0)
            eps4(0)
            for c in range(CHUNKS):
                norm4(0, c, normed[:, c])

            def qkv(c):
                if c >= 2:
                    dve.wait_ge(la_phiq, c - 1)
                dve.wait_ge(la_q, c + 1)
                ve.tensor_scalar(min_q[:, c % 2], ps[:, c % 2, :], bq_c, 0.0, ALU.add, ALU.min).then_inc(la_qmin, 1)
                if c >= 2:
                    dve.wait_ge(la_kexp, c - 1)
                    dve.wait_ge(la_sum, c - 1)
                dve.wait_ge(la_kv, c + 1)
                kb = 2 + 2 * (c % 2)
                kv = ps[:, kb:kb + 2, :].rearrange("p a (i n) -> p (a i) n", n=2 * P)
                ve.tensor_tensor(kz[:, c % 2].rearrange("p (i n) -> p i n", i=4), kv[:, :, 0:P],
                                 bkv[:, 0:1, :].broadcast_to([P, 4, P]), ALU.add).then_inc(la_kb, 1)
                ve.tensor_tensor(Vo[:, c % 2, :, 0:P], kv[:, :, P:],
                                 bkv[:, 1:2, :].broadcast_to([P, 4, P]), ALU.add).then_inc(la_v, 1)
                dve.wait_ge(la_kb, c + 1)
                if c >= 2:
                    dve.wait_ge(la_phik, c - 1)
                ve.tensor_scalar(min_k[:, c % 2], kz[:, c % 2], 0.0, None, ALU.min).then_inc(la_kmin, 1)

            def block_diagonal(b):
                dve.wait_ge(la_sum, CPB * (b + 1))
                ve.tensor_tensor(bd[:, b, 0], ps[:, 6 + b, 0:P], blocks, ALU.mult)
                ve.tensor_scalar(bd[:, b, 1], blocks, ps[:, 6 + b, P:P + 1], None, ALU.mult).then_inc(la_bd, 1)

            for c in range(CHUNKS):
                qkv(c)
                if c >= CPB:
                    block_diagonal(c - CPB)
            for c in range(CHUNKS):
                dve.wait_ge(la_den, c + 1)
                if c >= 2:
                    dve.wait_ge(la_att, c - 1)
                ve.tensor_scalar(rden[:, c % 2], ps[:, 2 + c % 2, :], LA_EPS, None, ALU.add).then_inc(la_eps, 1)
                dve.wait_ge(la_eps, c + 1)
                ve.reciprocal(rden[:, c % 2], rden[:, c % 2]).then_inc(la_rden, 1)
                dve.wait_ge(la_rden, c + 1)
                if c >= 2:
                    dve.wait_ge(la_y, c - 1)
                ve.tensor_tensor(att[:, c % 2], ps[:, c % 2, :], rden[:, c % 2], ALU.mult).then_inc(la_att, 1)
            eps4(1)
            for c in range(CHUNKS):
                if c >= 2:
                    dve.wait_ge(la_x1, c - 1)
                norm4(1, c, xn[:, c % 2])
                dve.wait_ge(l4_out, 4 + c + 1)
                xc = x1[:, c * CH:(c + 1) * CH]
                ve.tensor_tensor(xc, xc, xn[:, c % 2], ALU.add).then_inc(la_x1, 1)
            eps4(2)
            for c in range(CHUNKS):
                norm4(2, c, xin[:, ccol(c):ccol(c) + CH])
            dve.wait_ge(l4_out, 12)

            def shift(dst, src, col, width):
                ve.tensor_copy(dst[0:64, :], src[0:64, bass.ds(col, width)])
                return ve.tensor_copy(dst[64:P, :], src[64:P, bass.ds(col - 1, width)])

            def products(l, t, p, h):
                dve.wait_ge(sq_done[h], l * TILES + t + 2)
                if not (isinstance(t, int) and t == 0):
                    dve.wait_ge(tk_done[h], l * TILES + t)
                dve.wait_ge(add_done[h], l * TILES + t + 1)
                tab = rot_tab[:, bass.ds(t % TPB, 1), :, :].rearrange("p a s n -> p (a s) n")
                qk = ps[:, 0:2, :].rearrange("p a (h d) -> p a h d", d=HD)
                ve.tensor_tensor(rotA[:, p, h, :].rearrange("p (a h d) -> p a h d", a=2, d=HD), qk,
                                 tab[:, 0, :].rearrange("p (a d) -> p a d", a=2).unsqueeze(2).broadcast_to([P, 2, 8, HD]),
                                 ALU.mult)
                swapped = ps[:, 0:2, :].rearrange("p a (h x f) -> p (a h) x f", x=2, f=32)[:, :, ::-1, :]
                ve.tensor_tensor(rotB[:, h, :].rearrange("p (a h d) -> p a h d", a=2, d=HD), swapped,
                                 tab[:, 1, :].rearrange("p (a d) -> p a d", a=2).unsqueeze(2).broadcast_to([P, 2, 8, HD]),
                                 ALU.mult).then_inc(prod_done[h], 1)

            def square_sums(h):
                ve.tensor_reduce(nrm[:, h, :], sq[:, h, :].rearrange("p (a d) -> p a d", d=HD), AX.X,
                                 ALU.add).then_inc(nrm_done[h], 1)

            def guess(l, t):
                dve.wait_ge(nrm_done[1], l * TILES + t + 2)
                dve.wait_ge(r_done, l * TILES + t + 1)
                ve.tensor_scalar(nsq[:], nrm[:], L2_EPS * L2_EPS, None, ALU.max).then_inc(nsq_done, 1)
                dve.wait_ge(nsq_done, l * TILES + t + 2)
                ve.tensor_scalar(nhalf[:], nsq[:], -0.5, None, ALU.mult)
                ve.tensor_scalar(rinv[:].bitcast(I32), nsq[:].bitcast(I32), -0.5, RSQRT_BITS,
                                 ALU.mult, ALU.add).then_inc(guess_done, 1)

            def sums(l, t, p):
                dve.wait_ge(exp_done, l * TILES + t + 2)
                ve.tensor_reduce(ssum[:], prob[:, p], AX.X, ALU.add).then_inc(sum_done, 1)
                dve.wait_ge(sum_done, l * TILES + t + 2)
                ve.reciprocal(rsum[:], ssum[:]).then_inc(rs_done, 1)

            def build_xs(l, t, p):
                if not (isinstance(t, int) and t == 0):
                    dve.wait_ge(xlo_done, l * TILES + t)
                shift(xs[:, p, :], xin, tcol(t), P).then_inc(xs_done, 1)

            def spread(l, t, p, windows=range(NW)):
                if 0 in windows:
                    dve.wait_ge(norm_done, l * TILES + t + 2)
                    if not (isinstance(t, int) and t == 0):
                        dve.wait_ge(av_done[1], l * TILES + t)
                for w in windows:
                    q0 = WIN * w
                    ve.transpose(PT[q0:q0 + WIN, p, :, q0:q0 + WIN], prob[q0:q0 + WIN, p, :, WIN:])
                    if w:
                        last = ve.transpose(PT[q0 - WIN:q0, p, :, q0:q0 + WIN], prob[q0:q0 + WIN, p, :, 0:WIN])
                    else:
                        last = ve.transpose(PTp[P - WIN:P, p, :, 0:WIN], prob[0:WIN, p, :, 0:WIN])
                if NW - 1 in windows:
                    last.then_inc(pt_done, 1)

            def maxima(l, t, p):
                dve.wait_ge(s_done, l * TILES + t + 2)
                ve.tensor_reduce(mx[:], ps[:, 4:6, :].rearrange("p e (a n) -> p (e a) n", n=2 * WIN), AX.X,
                                 ALU.max).then_inc(mx_done, 1)
                dve.wait_ge(mx_done, l * TILES + t + 2)
                dve.wait_ge(r_done, l * TILES + t + 2)
                ve.scalar_tensor_tensor(mxn[:].rearrange("p (e h a) -> p e h a", e=2, h=2),
                                        mx[:].rearrange("p (e h a) -> p e h a", e=2, h=2), -1.0,
                                        rq[:, p, :, :].rearrange("p h (a e) -> p e h a", e=2),
                                        ALU.mult, ALU.mult).then_inc(mxn_done, 1)

            def residual(l, t):
                dve.wait_ge(y_done, l * TILES + t + 2)
                col = tcol(t)
                ve.tensor_tensor(xmid[:, bass.ds(col, P)], ps[:, Y_BANK, 0:P], xin[:, bass.ds(col, P)],
                                 ALU.add).then_inc(xmid_done, 1)

            def ffn_out(l, c):
                dve.wait_ge(f_done, l * CHUNKS + c + 2)
                col = ccol(c)
                ve.scalar_tensor_tensor(xin[:, col:col + CH], ps[:, 7, :], b2c[:], xmid[:, col:col + CH],
                                        ALU.add, ALU.add).then_inc(xout_done, 1)

            def shift_chunk(l, c):
                if c:
                    dve.wait_ge(ln_cen, l * CHUNKS + c + 1)
                shift(xsf, xmid, ccol(c), CH).then_inc(xsf_done, 1)

            def slot(l, s, p, qk, score, av, y, more):
                if qk:
                    products(l, s, p, 0)
                if y:
                    residual(l, s - 4)
                if qk:
                    square_sums(0)
                if more:
                    build_xs(l, s + 1, 1 - p)
                if av:
                    sums(l, s - 2, p)
                if qk:
                    products(l, s, p, 1)
                    square_sums(1)
                    guess(l, s)
                if av:
                    spread(l, s - 2, p, range(0, 1))
                if score:
                    maxima(l, s - 1, 1 - p)
                if av:
                    spread(l, s - 2, p, range(1, NW))

            def layer(l, more):
                slot(l, 1, 1, True, True, False, False, True)
                slot(l, 2, 0, True, True, True, False, True)
                slot(l, 3, 1, True, True, True, False, True)
                with dve.Fori(0, TILES // 2 - 3) as j:
                    for p in range(2):
                        slot(l, 2 * j + 4 + p, p, True, True, True, True, True)
                slot(l, TILES - 2, 0, True, True, True, True, True)
                slot(l, TILES - 1, 1, True, True, True, True, False)
                n = l * CHUNKS
                dve.wait_ge(s_wffn, l * N_WFFN + N_WFFN)
                dve.wait_ge(xmid_done, l * TILES + CH // P + 1)
                shift_chunk(l, 0)
                slot(l, TILES, 0, False, True, True, True, False)
                residual(l, TILES - 3)
                sums(l, TILES - 1, 1)
                ln_a(n)
                shift_chunk(l, 1)
                spread(l, TILES - 1, 1)
                ln_b(n, xn[:, 0, :])
                residual(l, TILES - 2)
                ln_a(n + 1)
                for c in range(CHUNKS):
                    head = more and c == CHUNKS - 1
                    if head:
                        dve.wait_ge(xout_done, l * CHUNKS + 2)
                        build_xs(l + 1, 0, 0)
                    for m, (_, fb) in enumerate(FBLK):
                        k = 3 * c + m
                        dve.wait_ge(gl_done, l * 12 + k + 2)
                        if m == 0 and c >= 2:
                            dve.wait_ge(f_done, l * CHUNKS + c)
                        ve.scalar_tensor_tensor(hm[0:fb, c % 2, m, :], ps[0:fb, 3 + k % 2, :], b1a[0:fb, m:m + 1],
                                                gl[0:fb, k % 2, :], ALU.add, ALU.mult).then_inc(hm_done, 1)
                        if c == 0 and m == 0:
                            residual(l, TILES - 1)
                        if m == 0 and c + 2 < CHUNKS:
                            shift_chunk(l, c + 2)
                        if m == 0 and 0 < c < CHUNKS - 1:
                            ln_a(n + c + 1)
                        if m == int(not more) and c:
                            ffn_out(l, c - 1)
                        if m == 0 and head:
                            dve.wait_ge(tab_done, l + 3)
                            products(l + 1, 0, 0, 0)
                        if m == 1 and c + 1 < CHUNKS:
                            ln_b(n + c + 1, xn[:, (c + 1) % 2, :])
                if more:
                    square_sums(0)
                    build_xs(l + 1, 1, 1)
                    products(l + 1, 0, 0, 1)
                    square_sums(1)
                ffn_out(l, CHUNKS - 1)
                if more:
                    guess(l + 1, 0)

            build_xs(0, 0, 0)
            dve.wait_ge(tab_done, 2)
            slot(0, 0, 0, True, False, False, False, True)
            with dve.Fori(0, DEPTH - 1) as l:
                layer(l, True)
            layer(DEPTH - 1, False)
            eps4(3)
            for c in range(CHUNKS):
                norm4(3, c, normed[:, c])
            for c in range(CHUNKS):
                dve.wait_ge(l4_out, 12 + c + 1)
                ve.tensor_tensor(normed[:, c], normed[:, c], x1[:, c * CH:(c + 1) * CH], ALU.add).then_inc(fin_add, 1)

        @block.tensor
        def _(pe):
            te = nc.tensor

            def mm(o, lhsT, rhs, start=True, stop=True, **kw):
                return te.matmul(o, lhsT, rhs, start=start, stop=stop, **kw)

            def tr(o, i):
                return te.matmul(o, i, ident, start=True, stop=True, is_transpose=True)

            def ln_a(l, c):
                pe.wait_ge(xsf_done, l * CHUNKS + c + 2)
                if c:
                    pe.wait_ge(ln_sq, l * CHUNKS + c + 1)
                mm(ps[:, 0, :], centre, xsf[:]).then_inc(ln_cen, 1)

            def ln_b(n):
                pe.wait_ge(ln_sq, n + 2)
                pe.wait_ge(ln_out, n + 1)
                for i in range(4):
                    ins = mm(ps[:, 1, i:i + 1], ln_sqb[:, i * P:(i + 1) * P], ones_m[:, 0:1])
                ins.then_inc(ln_var, 1)

            def ln_c(n):
                pe.wait_ge(ln_pow, n + 2)
                pe.wait_ge(ln_out, n + 1)
                for i in range(4):
                    ins = tr(ps[:, 1, i * P:(i + 1) * P], ln_r[:, i:i + 1].broadcast_to([P, P]))
                ins.then_inc(ln_bc, 1)

            def var4(k, c):
                pe.wait_ge(l4_sq, 4 * k + c + 1)
                for i in range(4):
                    j = 4 * c + i
                    ins = mm(ps[:, 2, j:j + 1], squares[c % 2][:, i * P:(i + 1) * P], ones_m[:, 0:1])
                ins.then_inc(l4_var, 1)

            def ln4(k, src, ready=None):
                for c in range(CHUNKS):
                    if ready:
                        pe.wait_ge(ready, c + 1)
                    if c >= 2:
                        var4(k, c - 2)
                    mm(ps[:, c % 2, :], centre, src(c)).then_inc(l4_cen, 1)
                var4(k, 2)
                var4(k, 3)
                pe.wait_ge(l4_pow, k + 1)
                for c in range(CHUNKS):
                    for i in range(4):
                        j = 4 * c + i
                        ins = tr(ps[:, 4 + c, i * P:(i + 1) * P], l4_r[:, j:j + 1].broadcast_to([P, P]))
                    ins.then_inc(l4_bc, 1)

            def x1_chunk(c):
                return x1[:, c * CH:(c + 1) * CH]

            pe.wait_ge(s_const, 48)
            pe.wait_ge(s_x, 64)
            for c in range(CHUNKS):
                for i in range(4):
                    ins = tr(ps[:, 4 + c, i * P:(i + 1) * P], x_rows[:, c, i, :])
                ins.then_inc(xT_done, 1)
            pe.wait_ge(s_wla, 64)
            for i in range(4):
                ins = tr(ps[:, 3, i * P:(i + 1) * P], wnat[:, i, :])
            ins.then_inc(wT_done, 1)
            ln4(0, x1_chunk, xT_copied)
            pe.wait_ge(wT_copied, 1)

            def sums(c):
                pe.wait_ge(la_phik, c + 1)
                for i in range(4):
                    ins = mm(ps[:, 6 + c // CPB, 0:P + 1], phiK[:, c % 2, i * P:(i + 1) * P], Vo[:, c % 2, i, 0:P + 1],
                             start=(c % CPB == 0 and i == 0), stop=(c % CPB == CPB - 1 and i == 3))
                ins.then_inc(la_sum, 1)

            for c in range(CHUNKS):
                pe.wait_ge(l4_out, 4 if c else 2)
                if c >= 2:
                    pe.wait_ge(la_qexp, c - 1)
                    pe.wait_ge(la_v, c - 1)
                mm(ps[:, c % 2, :], wT[:, 0, :], normed[:, c]).then_inc(la_q, 1)
                for i in range(4):
                    ins = mm(ps[:, 2 + 2 * (c % 2) + i // 2, (i % 2) * 256:(i % 2) * 256 + 256],
                             normed[:, c, i * P:(i + 1) * P], wT[:, 1:3, :].rearrange("p a n -> p (a n)"))
                ins.then_inc(la_kv, 1)
                if c:
                    sums(c - 1)
            sums(CHUNKS - 1)

            def project_la(c):
                pe.wait_ge(la_att, c + 1)
                if c >= 2:
                    pe.wait_ge(la_ysb, c - 1)
                mm(ps[:, 4 + c % 2, :], wT[:, 3, :], att[:, c % 2]).then_inc(la_y, 1)

            pe.wait_ge(la_qexp, CHUNKS)
            pe.wait_ge(la_v, CHUNKS)
            for c in range(CHUNKS):
                pe.wait_ge(la_bd, c // CPB + 1)
                pe.wait_ge(la_phiq, c + 1)
                if c >= 2:
                    project_la(c - 2)
                mm(ps[:, c % 2, :], bd[:, c // CPB, 0], phiQ[:, c])
                mm(ps[:, 2 + c % 2, :], bd[:, c // CPB, 1], phiQ[:, c]).then_inc(la_den, 1)
            project_la(2)
            project_la(3)
            ln4(1, lambda c: ysb[:, c], la_ysb)
            ln4(2, x1_chunk, la_x1)

            def split_mm(o, parts, col):
                mm(o, parts[:, 0, :], w_hi[:, col:col + HALF], stop=False)
                mm(o, parts[:, 0, :], w_lo[:, col:col + HALF], start=False, stop=False)
                return mm(o, parts[:, 1, :], w_hi[:, col:col + HALF], start=False)

            def qk(l, t, p, h):
                if h == 0:
                    pe.wait_ge(wlo_done, 3 * l + 4)
                    pe.wait_ge(xlo_done, l * TILES + t + 2)
                pe.wait_ge(prod_done[1 - h], l * TILES + t + h + 1)
                pe.wait_ge(sq_done[1 - h], l * TILES + t + h + 1)
                for a in range(2):
                    o = a * INNER + h * HALF
                    ins = split_mm(ps[:, a, :], x_hl[:, p], o)
                ins.then_inc(qk_done[h], 1)

            def tq(l, t, p, h):
                if h and not (isinstance(t, int) and t < 2):
                    pe.wait_ge(v_evac[1], l * TILES + t)
                pe.wait_ge(add_done[h], l * TILES + t + 2)
                for i in range(4):
                    ins = tr(ps[:, TQ_BANK[h], i * P:(i + 1) * P], rotA[:, p, h, i * P:(i + 1) * P])
                ins.then_inc(tq_done[h], 1)

            def tk(l, t, p, h):
                if h == 0:
                    pe.wait_ge(tq_evac[1], l * TILES + t + 2)
                elif not (isinstance(t, int) and t < 2):
                    pe.wait_ge(xmid_done, l * TILES + t - 1)
                pe.wait_ge(kmul_done, l * TILES + t + 2)
                for i in range(4):
                    ins = tr(ps[:, TK_BANK[h], i * P:(i + 1) * P], rotA[:, p, h, HALF + i * P:HALF + (i + 1) * P])
                ins.then_inc(tk_done[h], 1)

            def v(l, t, p, h):
                if h == 0:
                    pe.wait_ge(xsv_done, l * TILES + t + 2)
                    pe.wait_ge(o_evac[0], l * TILES + t + 1)
                o = 2 * INNER + h * HALF
                split_mm(ps[:, V_BANK[h], :], xsv[:, p], o).then_inc(v_done[h], 1)

            def scores(l, t):
                pe.wait_ge(exp_done, l * TILES + t + 1)
                for e in range(2):
                    if e:
                        pe.wait_ge(tk_evac[1], l * TILES + t + 2)
                    mm(ps[:, 4 + e, :], ident_b[:], mask[:, bass.ds(t, 1), :].broadcast_to([P, PAIRS, 2 * WIN]),
                       stop=False, skip_group_check=True)
                for a in range(PAIRS):
                    for w in range(NW):
                        for e in range(2):
                            ins = mm(ps[WIN * w:WIN * w + WIN, 4 + e, a * 64:a * 64 + 64],
                                     qT[64 * e:64 * e + 64, a, WIN * w:WIN * w + WIN],
                                     kT[64 * e:64 * e + 64, a, WIN * w:WIN * w + 2 * WIN],
                                     start=False, stop=True, skip_group_check=True)
                ins.then_inc(s_done, 1)

            def av(l, t, p, h):
                if h == 0:
                    pe.wait_ge(v_evac[1], l * TILES + t + 2)
                    pe.wait_ge(pt_done, l * TILES + t + 2)
                for i in range(4):
                    for e in range(2):
                        a = 4 * h + i
                        o = (2 * a + e) * HD
                        mm(ps[64 * e:64 * e + 64, O_BANK[h], i * P:(i + 1) * P], V[:, p, o:o + HD],
                           PT[:, p, e * PAIRS + a, :], start=(i == 0), skip_group_check=True)
                for i in range(4):
                    for e in range(2):
                        a = 4 * h + i
                        o = (2 * a + e) * HD
                        ins = mm(ps[64 * e:64 * e + 64, O_BANK[h], i * P:i * P + 2 * WIN], V[P - WIN:P, 1 - p, o:o + HD],
                                 PTp[P - WIN:P, p, e * PAIRS + a, :], start=False, skip_group_check=True)
                ins.then_inc(av_done[h], 1)

            def project(l, t):
                pe.wait_ge(o_evac[0], l * TILES + t + 2)
                pe.wait_ge(o_evac[1], l * TILES + t + 2)
                pe.wait_ge(xmid_done, l * TILES + t + 1)
                for a in range(PAIRS):
                    ins = mm(ps[:, Y_BANK, 0:P], wo[:, a, :], oT[:, a, :], start=(a == 0), stop=(a == PAIRS - 1))
                ins.then_inc(y_done, 1)

            def slot(l, s, p, score, av_v, o, has_qk=True, qk_next=True):
                if o:
                    av(l, s - 3, 1 - p, 0)
                if has_qk:
                    qk(l, s, p, 1)
                if score:
                    tk(l, s - 1, 1 - p, 0)
                    tk(l, s - 1, 1 - p, 1)
                if o:
                    av(l, s - 3, 1 - p, 1)
                if score:
                    scores(l, s - 1)
                if av_v:
                    v(l, s - 2, p, 0)
                    v(l, s - 2, p, 1)
                if qk_next:
                    qk(l, s + 1, 1 - p, 0)
                if o:
                    project(l, s - 3)
                if has_qk:
                    tq(l, s, p, 0)
                    tq(l, s, p, 1)

            def ffn_out(l, c):
                pe.wait_ge(hm_done, l * 12 + 3 * c + 4)
                if c:
                    pe.wait_ge(xout_done, l * CHUNKS + c + 1)
                for m, (o, fb) in enumerate(FBLK):
                    ins = mm(ps[:, 7, :], w2[0:fb, m, :], hm[0:fb, c % 2, m, :], start=(m == 0), stop=(m == 2))
                ins.then_inc(f_done, 1)

            pe.wait_ge(init_v, 4)
            pe.wait_ge(init_p, 3)
            def layer(l, more):
                slot(l, 1, 1, True, False, False)
                slot(l, 2, 0, True, True, False)
                with pe.Fori(0, TILES // 2 - 2) as j:
                    for i in range(2):
                        slot(l, 2 * j + 3 + i, 1 - i, True, True, True)
                slot(l, TILES - 1, 1, True, True, True, True, False)
                slot(l, TILES, 0, True, True, True, False, False)
                n = l * CHUNKS
                ln_a(l, 0)
                av(l, TILES - 2, 0, 0)
                av(l, TILES - 2, 0, 1)
                ln_b(n)
                v(l, TILES - 1, 1, 0)
                v(l, TILES - 1, 1, 1)
                project(l, TILES - 2)
                ln_c(n)
                ln_a(l, 1)
                av(l, TILES - 1, 1, 0)
                av(l, TILES - 1, 1, 1)
                ln_b(n + 1)
                pe.wait_ge(s_wffn, l * N_WFFN + N_WFFN)
                for c in range(CHUNKS):
                    for m, (o, fb) in enumerate(FBLK):
                        k = 3 * c + m
                        if m == 0:
                            pe.wait_ge(ln_out, n + c + 2)
                        if k == 1:
                            pe.wait_ge(xmid_done, l * TILES + TILES + 1)
                        if k >= 2:
                            pe.wait_ge(hm_done, l * 12 + k)
                        mm(ps[0:fb, 3 + k % 2, :], w1[:, o:o + fb], xn[:, c % 2, :])
                        mm(ps[0:fb, 5 + k % 2, :], w1[:, FF + o:FF + o + fb], xn[:, c % 2, :]).then_inc(h_done, 1)
                        if k == 0:
                            project(l, TILES - 1)
                            ln_c(n + 1)
                        if m == 0 and c:
                            ffn_out(l, c - 1)
                            if c + 1 < CHUNKS:
                                ln_b(n + c + 1)
                        if more and c == CHUNKS - 1 and m == 0:
                            pe.wait_ge(s_wattn, l * N_WATTN + 2 * N_WATTN)
                            qk(l + 1, 0, 0, 0)
                        if more and c == CHUNKS - 1 and m == 2:
                            qk(l + 1, 0, 0, 1)
                        if m == 1 and 0 < c < CHUNKS - 1:
                            ln_c(n + c + 1)
                        if m == 2 and c + 2 < CHUNKS:
                            ln_a(l, c + 2)
                ffn_out(l, CHUNKS - 1)
                if more:
                    qk(l + 1, 1, 1, 0)
                    tq(l + 1, 0, 0, 0)
                    tq(l + 1, 0, 0, 1)

            pe.wait_ge(s_wattn, N_WATTN)
            qk(0, 0, 0, 0)
            slot(0, 0, 0, False, False, False)
            with pe.Fori(0, DEPTH - 1) as l:
                layer(l, True)
            layer(DEPTH - 1, False)
            pe.wait_ge(xout_done, DEPTH * CHUNKS + 1)
            ln4(3, lambda c: xin[:, ccol(c):ccol(c) + CH])
            for c in range(CHUNKS):
                pe.wait_ge(fin_add, c + 1)
                for i in range(4):
                    ins = tr(ps[:, c, i * P:(i + 1) * P], normed[:, c, i * P:(i + 1) * P])
                ins.then_inc(fin_T, 1)


_INS = ['L0_attn_x', 'L0_attn_Wq', 'L0_attn_bq', 'L0_attn_Wk', 'L0_attn_bk', 'L0_attn_Wv', 'L0_attn_bv',
        'L0_attn_Wo', 'L0_attn_bo', 'L0_ffn_Wqkv', 'L0_ffn_q_scale', 'L0_ffn_k_scale', 'L0_ffn_Wo',
        'L0_ffn_ln_g', 'L0_ffn_ln_b', 'L0_ffn_W1', 'L0_ffn_b1', 'L0_ffn_W2', 'L0_ffn_b2']


def _constants():
    import numpy as np

    i = np.arange(P)
    mats = np.stack([np.eye(P), np.eye(P) - 1.0 / P, (i[:, None] // LA_HD == i[None, :] // LA_HD),
                     np.full((P, P), 1.0 / P)], 1).astype(np.float32)
    half = np.arange(0, HD, 2, dtype=np.float32)
    inv_freq = (np.float32(1.0) / np.float32(10000.0) ** (half / np.float32(HD))).astype(np.float32)
    pos = np.arange(N, dtype=np.float32)
    freqs = pos[:, None] * inv_freq[None, :]
    base = (half + np.float32(0.4 * HD)) / np.float32(1.4 * HD)
    power = (pos - N // 2) / np.float32(WIN // 2)
    scale = (base[None, :] ** power[:, None]).astype(np.float32)
    cos, sin = np.cos(freqs), np.sin(freqs)
    both = []
    for s in (scale, np.float32(1.0) / scale):
        both.append((np.concatenate([cos * s, cos * s], 1), np.concatenate([-sin * s, sin * s], 1)))
    rot = np.stack([np.concatenate([both[0][k], both[1][k]], 1) for k in range(2)], 1)
    rot = rot.reshape(TPB, P, 2, P).transpose(1, 0, 2, 3).astype(np.float32)
    q, j = np.arange(P)[:, None] % WIN, np.arange(2 * WIN)[None, :]
    seen = (j >= q) & (j <= q + WIN)
    first = seen & ~((np.arange(P)[:, None] < WIN) & (j < WIN))
    mask = np.where(np.stack([first, seen], 1), 0.0, -1e30).astype(np.float32)
    return {"c_mats": mats, "c_rot": rot, "c_mask": mask}


def kernel(**inputs):
    import numpy as np
    import concourse.bacc as bacc
    from concourse.bass_utils import run_bass_kernel_spmd

    nc = bacc.Bacc("TRN2", target_bir_lowering=False, num_devices=1)
    arrays, args = {}, []
    given = {name: np.ascontiguousarray(inputs[name]) for name in _INS}
    given.update({k: np.ascontiguousarray(a) for k, a in _constants().items()})
    for name, a in given.items():
        arrays[f"in_{name}"] = a
        args.append(nc.dram_tensor(f"in_{name}", a.shape, mybir.dt.from_np(a.dtype), kind="ExternalInput").ap())
    o = nc.dram_tensor("out_0", (B, N, P), F32, kind="ExternalOutput").ap()
    program(nc, *args, o)
    r = run_bass_kernel_spmd(nc, [arrays], core_ids=[0])
    return r.results[0]["out_0"]
```
